# Optimizing a Trainium2 kernel written in Bass

```python
import numpy as np
import jax
import jax.numpy as jnp

def _softmax(x, axis=-1):
    return jax.nn.softmax(x, axis=axis)

def _gelu(x):
    return jax.nn.gelu(x, approximate=True)

def _silu(x):
    return jax.nn.silu(x)

def _sigmoid(x):
    return jax.nn.sigmoid(x)

def _layernorm(x, axis=-1, eps=1e-05):
    m = jnp.mean(x, axis=axis, keepdims=True)
    v = jnp.var(x, axis=axis, keepdims=True)
    return (x - m) / jnp.sqrt(v + eps)

def _scatter_add(tgt, idx, src, axis=0):
    return tgt.at[idx].add(src)

def _segment_sum(src, seg, n):
    return jax.ops.segment_sum(src, seg, n)
kernel_name = 'mk_vit_tower_d1_tok_img1024_r4_c116bf'

def setup_inputs(seed: int=0):
    np.random.seed(seed)
    _w = jnp.asarray

    def _rec_inputs():
        import jax
        import jax.numpy as jnp
        _rk = jax.random.key(seed)
        x = -0.000222058 + 0.999998 * jax.random.normal(jax.random.fold_in(_rk, 1), (64, 3, 64, 64), jnp.float32)
        return x
    x = _rec_inputs()

    def _L0_tok_setup():
        import jax, jax.numpy as jnp
        import numpy as np
        IMG, PS, C, OUT = (64, 16, 3, 256)
        NP = IMG // PS
        IN_FEAT = C * PS * PS
        key = jax.random.key(seed)
        k1, k2, k3, k4 = jax.random.split(key, 4)
        x = jax.random.normal(k1, (128, C, IMG, IMG), dtype=jnp.float32)
        W = jax.random.normal(k2, (OUT, IN_FEAT), dtype=jnp.float32) / np.sqrt(IN_FEAT)
        b = jax.random.normal(k3, (OUT,), dtype=jnp.float32) * 0.01
        pos_emb = jax.random.normal(k4, (NP * NP, OUT), dtype=jnp.float32)
        return {'x': x, 'W': W, 'b': b, 'pos_emb': pos_emb}
    _L0_tok_all = _L0_tok_setup()
    _L0_tok_in = {k: v for k, v in _L0_tok_all.items() if k in ('W', 'b', 'pos_emb')}
    del _L0_tok_all

    def _L0_attn_setup():
        import jax, jax.numpy as jnp
        import numpy as np
        D_MODEL = 256
        N_HEADS = 16
        HEAD_DIM = D_MODEL // N_HEADS
        KV_LATENT = 64
        LN_EPS = 1e-05

        def apply_rope(x):
            b, h, t, d = x.shape
            half = d // 2
            pos = jnp.arange(t, dtype=x.dtype)[:, None]
            inv_freq = 1.0 / 10000.0 ** (jnp.arange(half, dtype=x.dtype) / half)
            angles = pos * inv_freq[None, :]
            sin = jnp.sin(angles)[None, None]
            cos = jnp.cos(angles)[None, None]
            x1, x2 = (x[..., :half], x[..., half:])
            return jnp.concatenate([x1 * cos - x2 * sin, x1 * sin + x2 * cos], axis=-1)
        key = jax.random.key(seed)
        ks = jax.random.split(key, 6)
        d, L = (D_MODEL, KV_LATENT)
        s = 1.0 / np.sqrt(d)
        sl = 1.0 / np.sqrt(L)
        return {'x': jax.random.normal(ks[0], (2, 512, d), dtype=jnp.float32), 'W_q': jax.random.uniform(ks[1], (d, d), jnp.float32, -s, s), 'W_dkv': jax.random.uniform(ks[2], (d, L), jnp.float32, -s, s), 'W_uk': jax.random.uniform(ks[3], (L, d), jnp.float32, -sl, sl), 'W_uv': jax.random.uniform(ks[4], (L, d), jnp.float32, -sl, sl), 'W_o': jax.random.uniform(ks[5], (d, d), jnp.float32, -s, s), 'ln_gamma': jnp.ones((L,), jnp.float32), 'ln_beta': jnp.zeros((L,), jnp.float32)}
    _L0_attn_all = _L0_attn_setup()
    _L0_attn_in = {k: v for k, v in _L0_attn_all.items() if k in ('W_q', 'W_dkv', 'W_uk', 'W_uv', 'W_o', 'ln_gamma', 'ln_beta')}
    del _L0_attn_all

    def _L0_ffn_setup():
        import jax, jax.numpy as jnp
        import numpy as np
        DIM = 256
        INTER = 256
        N_EXPERTS = 8
        TOPK = 2
        N_SHARED = 2
        key = jax.random.key(seed)
        ks = jax.random.split(key, 10)
        s = 0.02
        return {'x': jax.random.normal(ks[0], (4, 512, DIM), dtype=jnp.float32), 'gate_w': jax.random.normal(ks[1], (N_EXPERTS, DIM), dtype=jnp.float32) * s, 'gate_bias': jax.random.normal(ks[2], (N_EXPERTS,), dtype=jnp.float32) * s, 'w1': jax.random.normal(ks[3], (N_EXPERTS, INTER, DIM), dtype=jnp.float32) * s, 'w3': jax.random.normal(ks[4], (N_EXPERTS, INTER, DIM), dtype=jnp.float32) * s, 'w2': jax.random.normal(ks[5], (N_EXPERTS, DIM, INTER), dtype=jnp.float32) * s, 'sw1': jax.random.normal(ks[6], (N_SHARED * INTER, DIM), dtype=jnp.float32) * s, 'sw3': jax.random.normal(ks[7], (N_SHARED * INTER, DIM), dtype=jnp.float32) * s, 'sw2': jax.random.normal(ks[8], (DIM, N_SHARED * INTER), dtype=jnp.float32) * s}
    _L0_ffn_all = _L0_ffn_setup()
    _L0_ffn_in = {k: v for k, v in _L0_ffn_all.items() if k in ('gate_w', 'gate_bias', 'w1', 'w3', 'w2', 'sw1', 'sw3', 'sw2')}
    del _L0_ffn_all
    return {'x': x, 'L0_tok_W': _L0_tok_in['W'], 'L0_tok_b': _L0_tok_in['b'], 'L0_tok_pos_emb': _L0_tok_in['pos_emb'], 'L0_attn_W_q': _L0_attn_in['W_q'], 'L0_attn_W_dkv': _L0_attn_in['W_dkv'], 'L0_attn_W_uk': _L0_attn_in['W_uk'], 'L0_attn_W_uv': _L0_attn_in['W_uv'], 'L0_attn_W_o': _L0_attn_in['W_o'], 'L0_attn_ln_gamma': _L0_attn_in['ln_gamma'], 'L0_attn_ln_beta': _L0_attn_in['ln_beta'], 'L0_ffn_gate_w': _L0_ffn_in['gate_w'], 'L0_ffn_gate_bias': _L0_ffn_in['gate_bias'], 'L0_ffn_w1': _L0_ffn_in['w1'], 'L0_ffn_w3': _L0_ffn_in['w3'], 'L0_ffn_w2': _L0_ffn_in['w2'], 'L0_ffn_sw1': _L0_ffn_in['sw1'], 'L0_ffn_sw3': _L0_ffn_in['sw3'], 'L0_ffn_sw2': _L0_ffn_in['sw2']}

def reference(x, L0_tok_W, L0_tok_b, L0_tok_pos_emb, L0_attn_W_q, L0_attn_W_dkv, L0_attn_W_uk, L0_attn_W_uv, L0_attn_W_o, L0_attn_ln_gamma, L0_attn_ln_beta, L0_ffn_gate_w, L0_ffn_gate_bias, L0_ffn_w1, L0_ffn_w3, L0_ffn_w2, L0_ffn_sw1, L0_ffn_sw3, L0_ffn_sw2):
    import jax
    import jax.numpy as jnp

    def _L0_tok_ref(x, W, b, pos_emb):
        import jax, jax.numpy as jnp
        import numpy as np
        IMG, PS, C, OUT = (64, 16, 3, 256)
        NP = IMG // PS
        IN_FEAT = C * PS * PS
        B = x.shape[0]
        p = x.reshape(B, C, NP, PS, NP, PS).transpose(0, 1, 2, 4, 3, 5)
        p = p.transpose(0, 2, 3, 1, 4, 5)
        p = p.reshape(B, NP * NP, IN_FEAT)
        out = jnp.einsum('bnf,of->bno', p, W) + b + pos_emb
        return out

    def _L0_attn_ref(x, W_q, W_dkv, W_uk, W_uv, W_o, ln_gamma, ln_beta):
        import jax, jax.numpy as jnp
        import numpy as np
        D_MODEL = 256
        N_HEADS = 16
        HEAD_DIM = D_MODEL // N_HEADS
        KV_LATENT = 64
        LN_EPS = 1e-05

        def apply_rope(x):
            b, h, t, d = x.shape
            half = d // 2
            pos = jnp.arange(t, dtype=x.dtype)[:, None]
            inv_freq = 1.0 / 10000.0 ** (jnp.arange(half, dtype=x.dtype) / half)
            angles = pos * inv_freq[None, :]
            sin = jnp.sin(angles)[None, None]
            cos = jnp.cos(angles)[None, None]
            x1, x2 = (x[..., :half], x[..., half:])
            return jnp.concatenate([x1 * cos - x2 * sin, x1 * sin + x2 * cos], axis=-1)
        b, t, _ = x.shape
        q = (x @ W_q).reshape(b, t, N_HEADS, HEAD_DIM).transpose(0, 2, 1, 3)
        lat = x @ W_dkv
        mu = jnp.mean(lat, axis=-1, keepdims=True)
        var = jnp.mean(jnp.square(lat - mu), axis=-1, keepdims=True)
        lat = (lat - mu) * jax.lax.rsqrt(var + LN_EPS) * ln_gamma + ln_beta
        k = (lat @ W_uk).reshape(b, t, N_HEADS, HEAD_DIM).transpose(0, 2, 1, 3)
        v = (lat @ W_uv).reshape(b, t, N_HEADS, HEAD_DIM).transpose(0, 2, 1, 3)
        q = apply_rope(q)
        k = apply_rope(k)
        scores = jnp.einsum('bhqd,bhkd->bhqk', q, k) / jnp.sqrt(jnp.float32(HEAD_DIM))
        causal = jnp.tril(jnp.ones((t, t), dtype=bool))
        scores = jnp.where(causal[None, None], scores, -jnp.inf)
        attn = jax.nn.softmax(scores, axis=-1)
        out = jnp.einsum('bhqk,bhkd->bhqd', attn, v)
        out = out.transpose(0, 2, 1, 3).reshape(b, t, D_MODEL)
        return out @ W_o

    def _L0_ffn_ref(x, gate_w, gate_bias, w1, w3, w2, sw1, sw3, sw2):
        import jax, jax.numpy as jnp
        import numpy as np
        DIM = 256
        INTER = 256
        N_EXPERTS = 8
        TOPK = 2
        N_SHARED = 2
        shape = x.shape
        xt = x.reshape(-1, shape[-1])
        scores = jax.nn.softmax((xt @ gate_w.T).astype(jnp.float32), axis=-1)
        _, idx = jax.lax.top_k(scores + gate_bias, TOPK)
        weights = jnp.take_along_axis(scores, idx, axis=1).astype(x.dtype)
        y = jnp.zeros_like(xt)
        for e in range(N_EXPERTS):
            gate_e = jnp.sum(jnp.where(idx == e, weights, 0.0), axis=1)
            h = jax.nn.silu(xt @ w1[e].T) * (xt @ w3[e].T)
            y = y + gate_e[:, None] * (h @ w2[e].T)
        z = jax.nn.silu(xt @ sw1.T) * (xt @ sw3.T) @ sw2.T
        return (y + z).reshape(shape)
    h = _L0_tok_ref(x, L0_tok_W, L0_tok_b, L0_tok_pos_emb)
    h = h + _L0_attn_ref(_layernorm(h, axis=-1), L0_attn_W_q, L0_attn_W_dkv, L0_attn_W_uk, L0_attn_W_uv, L0_attn_W_o, L0_attn_ln_gamma, L0_attn_ln_beta)
    h = h + _L0_ffn_ref(_layernorm(h, axis=-1), L0_ffn_gate_w, L0_ffn_gate_bias, L0_ffn_w1, L0_ffn_w3, L0_ffn_w2, L0_ffn_sw1, L0_ffn_sw3, L0_ffn_sw2)
    return h

_drawn_inputs = setup_inputs


def setup_inputs(seed=0):
    import zlib

    import numpy as np

    out = dict(_drawn_inputs(seed))
    spreads = {'L0_attn_ln_gamma': (1.0, 0.6), 'L0_attn_ln_beta': (0.0, 0.337)}
    factors = {'L0_tok_b': 7.317,
     'L0_ffn_gate_w': 8.0,
     'L0_ffn_gate_bias': 8.0,
     'L0_ffn_w1': 8.0,
     'L0_ffn_w3': 8.0,
     'L0_ffn_w2': 8.0,
     'L0_ffn_sw1': 3.419,
     'L0_ffn_sw3': 3.392,
     'L0_ffn_sw2': 3.357}
    for name, (base, spread) in spreads.items():
        noise = np.random.default_rng([zlib.crc32(name.encode()), seed]).standard_normal(out[name].shape)
        drawn = base * np.exp(spread * noise) if base else spread * noise
        out[name] = jnp.asarray(drawn.astype(out[name].dtype))
    for name, factor in factors.items():
        out[name] = (out[name] * factor).astype(out[name].dtype)
    return out
```

```python
from contextlib import ExitStack

import numpy as np

import concourse.bass as bass
from concourse import mybir

F32 = mybir.dt.float32
I32 = mybir.dt.int32
ALU = mybir.AluOpType
ACT = mybir.ActivationFunctionType
AX = mybir.AxisListType

P = 128
IMAGES, CH, IMG, PS = 64, 3, 64, 16
NP = IMG // PS
T = NP * NP
D = 256
KD = D // P
FEAT = CH * PS * PS
KF = FEAT // P
HEADS, HD = 16, 16
HALF = 2
HPH = HEADS // HALF
LAT = 64
TOKENS = IMAGES * T
TILES = TOKENS // P
IPT = P // T
E, INTER, TOPK = 8, 256, 2
KI = INTER // P
SINTER = 2 * INTER
KS = SINTER // P
SLOT_TILES = TOKENS * TOPK // P + E
EPS = 1e-5
RING = 4
BLOCKS = SLOT_TILES // RING

C_ID = 0
C_TRI = C_ID + P
C_ONE = C_TRI + P
C_CQ = C_ONE + P
C_SQ = C_CQ + HD
C_CK = C_SQ + HD
C_SK = C_CK + HD
C_CAUSAL = C_SK + HD
C_LT = C_CAUSAL + T
C_THR = C_LT + E * E
C_TILE = C_THR + E
C_MHALF = C_TILE + SLOT_TILES
C_END = C_MHALF + 1
R_POS = 0
R_B = R_POS + D
R_GAM = R_B + D
R_BET = R_GAM + LAT
R_BIAS = R_BET + LAT
R_END = R_BIAS + E


def bc(ap, n, at):
    pairs = [list(x) for x in ap.ap]
    shape = list(ap.shape)
    out = ap.unsqueeze(at)
    shape.insert(at, n)
    return out.broadcast_to(shape)


def later(i):
    return not isinstance(i, int) or i > 0


def build(nc, xp, w_emb, w_qd, w_kv, w_o, w_gate, w_s13, w_s2, w_e13, w_e2, rows, consts, meta0, table0, out):
    ctx = ExitStack()
    with ctx:
        def sb(name, shape, dt=F32):
            return ctx.enter_context(nc.sbuf_tensor(name, shape, dt))

        def sem(name):
            return ctx.enter_context(nc.semaphore(name))

        bank = [ctx.enter_context(nc.psum_tensor(f"bank{i}", [P, 512], F32)) for i in range(8)]

        xn_rows = nc.dram_tensor("xn_rows", (TOKENS, D), F32).ap()
        table = nc.dram_tensor("slot_table", (P * SLOT_TILES, 4), I32).ap()
        y_rows = nc.dram_tensor("y_rows", (TOKENS * TOPK + P * SLOT_TILES, D), F32).ap()

        wemb = sb("wemb", [P, KF, D])
        wqd = sb("wqd", [P, KD, D + LAT])
        wkv = sb("wkv", [LAT, 2 * D])
        wo = sb("wo", [P, KD, D])
        wg = sb("wg", [P, KD, E])
        ws13 = sb("ws13", [P, KD, 2 * SINTER])
        ws2 = sb("ws2", [P, KS, D])
        we13 = sb("we13", [P, E, KD * 2 * INTER])
        we2 = sb("we2", [P, E, KI * D])
        cst = sb("cst", [P, C_END])
        row = sb("row", [P, R_END])
        ident = cst[:, C_ID:C_ID + P]
        xt = [sb(f"xt{u}", [P, KF, P]) for u in (0, 1)]
        posb = sb("posb", [P, D])
        h = [sb(f"h{u}", [P, D]) for u in (0, 1)]
        st = [sb(f"st{u}", [P, 40]) for u in (0, 1)]
        xn = [sb(f"xn{u}", [P, D]) for u in (0, 1)]
        xnT = [sb(f"xnT{u}", [P, KD, P]) for u in (0, 1)]
        qc = [sb(f"qc{u}", [P, D]) for u in (0, 1)]
        qs = [sb(f"qs{u}", [P, D]) for u in (0, 1)]
        qr = [sb(f"qr{u}", [P, D]) for u in (0, 1)]
        kc = [sb(f"kc{u}", [P, D]) for u in (0, 1)]
        ks = [sb(f"ks{u}", [P, D]) for u in (0, 1)]
        kr = [sb(f"kr{u}", [P, D]) for u in (0, 1)]
        lat = [sb(f"lat{u}", [P, LAT]) for u in (0, 1)]
        latg = [sb(f"latg{u}", [P, LAT]) for u in (0, 1)]
        latT = [sb(f"latT{u}", [LAT, P]) for u in (0, 1)]
        qT = [sb(f"qT{u}", [P, HALF, P]) for u in (0, 1)]
        kT = [sb(f"kT{u}", [P, HALF, P]) for u in (0, 1)]
        vT = [sb(f"vT{u}", [P, HALF, P]) for u in (0, 1)]
        kx = [sb(f"kx{u}", [P, HALF, HPH, P]) for u in (0, 1)]
        vxT = [sb(f"vxT{u}", [P, HALF, HPH, P]) for u in (0, 1)]
        vx = [sb(f"vx{u}", [P, IPT * HALF, P]) for u in (0, 1)]
        sT = [sb(f"sT{u}", [P, HALF, P]) for u in (0, 1)]
        sc = [sb(f"sc{u}", [P, D]) for u in (0, 1)]
        pr = [sb(f"pr{u}", [P, D]) for u in (0, 1)]
        sx = [sb(f"sx{u}", [P, 3, HEADS]) for u in (0, 1)]
        pT = [sb(f"pT{u}", [P, HALF, P]) for u in (0, 1)]
        oT = [sb(f"oT{u}", [P, KD, P]) for u in (0, 1)]
        h2 = [sb(f"h2{u}", [P, D]) for u in (0, 1)]
        xn2 = [sb(f"xn2{u}", [P, D]) for u in (0, 1)]
        xn2T = [sb(f"xn2T{u}", [P, KD, P]) for u in (0, 1)]
        th = [sb(f"th{u}", [P, SINTER]) for u in (0, 1)]
        hs = [sb(f"hs{u}", [P, SINTER]) for u in (0, 1)]
        hsT = [sb(f"hsT{u}", [P, KS, P]) for u in (0, 1)]
        acc = sb("acc", [P, TILES, D])
        lg = sb("lg", [P, TILES, E])
        G = TILES * E
        rt = sb("rt", [P, 8, G])
        r5 = vx[1][:, 0:4, :].rearrange("p a b -> p (a b)")
        r6 = vx[1][:, 4:8, :].rearrange("p a b -> p (a b)")
        isk = sb("isk", [P, TOPK, G])
        sml = sb("sml", [P, 8, E])
        kk = sb("kk", [P, TOPK * G])
        kv = sb("kv", [P, 2, TOPK * TILES])
        ki = sb("ki", [P, 4, TOPK * TILES], I32)
        tl = sb("tl", [P, SLOT_TILES * E])
        tf = sb("tf", [P, SLOT_TILES])
        ti = sb("ti", [P, SLOT_TILES], I32)
        meta = sb("meta", [P, TOPK * TILES, 4], I32)
        tb = sb("tb", [P, SLOT_TILES, 4], I32)
        def part(t, r, n):
            return t[:].rearrange("p a b c -> p (a b c)")[:, r * n:(r + 1) * n]

        xg = [part(vxT[0], r, D) for r in range(RING)]
        vx0 = vx[0][:].rearrange("p a b -> p (a b)")
        xgT, et, eh, ehT = ([vx0[:, (2 * n + r) * D:(2 * n + r + 1) * D] for r in (0, 1)] for n in range(4))
        ye = [part(vxT[1], r, D) for r in range(RING)]
        yg = [part(kx[0], r, TOPK * D).rearrange("p (k d) -> p k d", k=TOPK) for r in range(4)]
        fin = [part(kx[1], r, D) for r in range(4)]

        names = """ld_const ld_emb ld_qd ld_kv ld_o ld_s ld_e ld_init x_in0 x_in1 zeroed posb_ok
            emb h_ok h_stat h_aggr h_var h_rstd xn_ok xnT_ps xnT_ok qlat
            qc_ok qs_ok qr_ok l_stat l_aggr l_var l_rstd l_norm l_gam lat_ok latT_ps latT_ok qT_ps qT_ok
            k_ps kc_ok ks_ok kr_ok vT_ps vT_ok kT_ps kT_ok kx0 kx1 vx0 vx1 vx_ps vx_ok
            sT_ps sT_ok s_ps s_mask s_max s_sub s_exp s_sum s_rec p_ok pT_ps pT_ok oT_ps oT_ok o_ps h2_ok
            h2_stat h2_aggr h2_var h2_rstd xn2_ok xn2T_ps xn2T_ok xn2_out g_ps lg_ok
            sh_ps sh_tanh sh_gate sh_ok hsT_ps hsT_ok z_ps acc_ok
            route d_max d_exp cnt_ps routed scattered tab_in et_ok
            gat0 gat1 gat2 gat3 xgT_ps xgT_ok eh_ps e_tanh e_gate eh_ok ehT_ps ehT_ok y_ps y_ok
            sct0 sct1 sct2 sct3 yg0 yg1 yg2 yg3 f_add f_ok out0 out1 out2 out3""".split()
        s = {n: sem(n) for n in names}
        x_in = (s["x_in0"], s["x_in1"])
        kx_in = (s["kx0"], s["kx1"])
        vx_in = (s["vx0"], s["vx1"])
        gat = [s[f"gat{r}"] for r in range(RING)]
        sct = [s[f"sct{r}"] for r in range(RING)]
        yg_in = [s[f"yg{r}"] for r in range(4)]
        out_s = [s[f"out{r}"] for r in range(4)]

        block = ctx.enter_context(nc.Block())

        def heads(ap):
            return ap.rearrange("p (h j d) -> p h j d", h=HEADS, j=2)

        @block.sync
        def _(sp):
            sp.dma_start(cst[:], consts).then_inc(s["ld_const"], 16)
            sp.dma_start(row[:], rows).then_inc(s["ld_const"], 16)
            sp.dma_start(wqd[:], w_qd).then_inc(s["ld_qd"], 16)
            sp.dma_start(wkv[:], w_kv).then_inc(s["ld_kv"], 16)
            sp.dma_start(wo[:], w_o).then_inc(s["ld_o"], 16)
            sp.dma_start(wg[:], w_gate).then_inc(s["ld_o"], 16)
            sp.dma_start(table, table0).then_inc(s["ld_init"], 16)
            sp.dma_start(meta[:], meta0).then_inc(s["ld_init"], 16)
            def pair(i):
                for u in (0, 1):
                    sp.wait_ge(s["kT_ok"], 2 * i + u + 1)
                    if later(i):
                        sp.wait_ge(s["sT_ps"], 2 * i)
                    sp.wait_ge(s["zeroed"], 4)
                    for hd in range(HPH):
                        sp.dma_start(kx[u][hd * HD:(hd + 1) * HD, :, hd, :],
                                     kT[u][hd * HD:(hd + 1) * HD, :, :]).then_inc(kx_in[u], 16)
                    sp.wait_ge(s["vT_ok"], 2 * i + u + 1)
                    if later(i):
                        sp.wait_ge(s["s_ps"], 2 * i)
                    for hd in range(HPH):
                        sp.dma_start(vxT[u][hd * HD:(hd + 1) * HD, :, hd, :],
                                     vT[u][hd * HD:(hd + 1) * HD, :, :]).then_inc(vx_in[u], 16)
                for u in (0, 1):
                    sp.wait_ge(s["zeroed"], 4)
                    sp.wait_ge(s["xn2_ok"], 2 * i + u + 1)
                    sp.dma_start(xn_rows[bass.ds((2 * i + u) * P, P), :], xn2[u][:]).then_inc(s["xn2_out"], 16)

            pair(0)
            with sp.Fori(1, TILES // 2) as i:
                pair(i)
            sp.wait_ge(s["scattered"], 16 * TOPK * TILES)
            sp.dma_start(tb[:], table.rearrange("(p j) c -> p j c", p=P)).then_inc(s["tab_in"], 16)
            for r in range(RING):
                sp.wait_ge(sct[r], 16 * BLOCKS)
            y_tok = y_rows[0:TOKENS * TOPK, :].rearrange("(g p k) d -> g p (k d)", p=P, k=TOPK)
            for g in range(TILES):
                if g >= 4:
                    sp.wait_ge(s["f_ok"], g - 3)
                sp.dma_start(yg[g % 4].rearrange("p k d -> p (k d)"), y_tok[g]).then_inc(yg_in[g % 4], 16)
            for r in range(4):
                sp.wait_ge(out_s[r], 16 * TILES // 4)

        @block.gpsimd
        def _(pool):
            nc.gpsimd.memset(vxT[0][:], 0.0).then_inc(s["zeroed"], 1)
            nc.gpsimd.memset(vxT[1][:], 0.0).then_inc(s["zeroed"], 1)

            def rstd(u, g, src, ready, done):
                pool.wait_ge(s[ready], g + 1)
                nc.gpsimd.tensor_tensor(st[u][:, src + 1:src + 2], st[u][:, src:src + 1], cst[:, C_MHALF:C_MHALF + 1],
                                        ALU.pow).then_inc(s[done], 1)

            pool.wait_ge(s["ld_const"], 32)

            def pair(i):
                for u in (0, 1):
                    rstd(u, 2 * i + u, 8, "h_var", "h_rstd")
                for u in (0, 1):
                    rstd(u, 2 * i + u, 20, "l_var", "l_rstd")
                for c, sn, r, cok, sok, done, used in ((qc, qs, qr, "qc_ok", "qs_ok", "qr_ok", "qT_ps"),
                                                       (kc, ks, kr, "kc_ok", "ks_ok", "kr_ok", "kT_ps")):
                    for u in (0, 1):
                        pool.wait_ge(s[cok], 2 * i + u + 1)
                        pool.wait_ge(s[sok], 2 * i + u + 1)
                        if later(i):
                            pool.wait_ge(s[used], 2 * i)
                        for j in (0, 1):
                            nc.gpsimd.tensor_tensor(heads(r[u][:])[:, :, j, :], heads(c[u][:])[:, :, j, :],
                                                    heads(sn[u][:])[:, :, 1 - j, :], ALU.add).then_inc(s[done], 1)
                for u in (0, 1):
                    rstd(u, 2 * i + u, 32, "h2_var", "h2_rstd")

            pair(0)
            with pool.Fori(1, TILES // 2) as i:
                pair(i)
            pool.wait_ge(s["routed"], 1)
            pool.wait_ge(s["ld_init"], 32)
            for c in range(TOPK * TILES):
                nc.gpsimd.indirect_dma_start(
                    out=table, out_offset=bass.IndirectOffsetOnAxis(ap=ki[:, 3, c:c + 1], axis=0),
                    in_=meta[:, c, :], in_offset=None).then_inc(s["scattered"], 16)
            pool.wait_ge(s["tab_in"], 16)
            pool.wait_ge(s["xn2_out"], 16 * TILES)

            def gather(j):
                nc.gpsimd.indirect_dma_start(
                    out=xg[j % RING], out_offset=None, in_=xn_rows,
                    in_offset=bass.IndirectOffsetOnAxis(ap=tb[:, j, 0:1], axis=0)).then_inc(gat[j % RING], 16)

            for j in range(RING):
                gather(j)
            for j in range(SLOT_TILES):
                if j + RING < SLOT_TILES:
                    pool.wait_ge(s["xgT_ps"], j + 1)
                    gather(j + RING)
                pool.wait_ge(s["y_ok"], j + 1)
                nc.gpsimd.indirect_dma_start(
                    out=y_rows, out_offset=bass.IndirectOffsetOnAxis(ap=tb[:, j, 1:2], axis=0),
                    in_=ye[j % RING], in_offset=None).then_inc(sct[j % RING], 16)

        @block.scalar
        def _(act):
            act.dma_start(xt[0][:], xp[0]).then_inc(x_in[0], 16)
            act.dma_start(wemb[:], w_emb).then_inc(s["ld_emb"], 16)
            act.dma_start(xt[1][:], xp[1]).then_inc(x_in[1], 16)
            act.dma_start(ws13[:], w_s13).then_inc(s["ld_s"], 16)
            act.dma_start(ws2[:], w_s2).then_inc(s["ld_s"], 16)
            for e in range(E):
                act.dma_start(we13[:, e, :], w_e13[e]).then_inc(s["ld_e"], 16)
                act.dma_start(we2[:, e, :], w_e2[e]).then_inc(s["ld_e"], 16)

            def copy(dst, src, ready, at, done):
                act.wait_ge(s[ready], at)
                nc.scalar.copy(dst, src).then_inc(s[done], 1)

            def flat(t):
                return t[:].rearrange("p a b -> p (a b)")

            def images_first(t):
                return t[:, 0:D].rearrange("p (f i k) -> p f i k", f=HALF, i=IPT)

            def keys_first(t):
                return t[:].rearrange("p f (k i) -> p f i k", i=IPT)

            def attention(i, more):
                g = [2 * i, 2 * i + 1]
                for u in (0, 1):
                    copy(flat(xnT[u]), bank[4 * u + 1][:, 0:D], "xnT_ps", g[u] + 1, "xnT_ok")
                    if more:
                        act.wait_ge(s["emb"], g[u] + 1)
                        act.dma_start(xt[u][:], xp[g[u] + 2]).then_inc(x_in[u], 16)
                for u in (0, 1):
                    copy(latT[u][:], bank[4 * u + 3][0:LAT, 0:P], "latT_ps", g[u] + 1, "latT_ok")
                for u in (0, 1):
                    if later(i):
                        act.wait_ge(vx_in[u], P * i)
                    copy(keys_first(vT[u]), images_first(bank[4 * u + 1]), "vT_ps", g[u] + 1, "vT_ok")
                    copy(flat(qT[u]), bank[4 * u + 3][:, 0:D], "qT_ps", g[u] + 1, "qT_ok")
                for u in (0, 1):
                    if later(i):
                        act.wait_ge(kx_in[u], P * i)
                    copy(keys_first(kT[u]), images_first(bank[4 * u + 2]), "kT_ps", g[u] + 1, "kT_ok")
                for u in (0, 1):
                    copy(flat(sT[u]), bank[4 * u + 0][:, 0:D], "sT_ps", g[u] + 1, "sT_ok")
                for u in (0, 1):
                    for r in range(4):
                        copy(vx[u][:, 4 * r:4 * r + 4, :].rearrange("p a b -> p (a b)"), bank[4 * u + 1 + 2 * (r % 2)][:],
                             "vx_ps", 4 * g[u] + r + 1, "vx_ok")
                for u in (0, 1):
                    act.wait_ge(s["s_sub"], g[u] + 1)
                    nc.scalar.activation(sc[u][:], sc[u][:], ACT.Exp).then_inc(s["s_exp"], 1)
                for u in (0, 1):
                    copy(flat(pT[u]), bank[4 * u + 0][:, 0:D], "pT_ps", g[u] + 1, "pT_ok")
                for u in (0, 1):
                    copy(flat(oT[u]), bank[4 * u + 2][:, 0:D], "oT_ps", g[u] + 1, "oT_ok")
                for u in (0, 1):
                    copy(flat(xn2T[u]), bank[4 * u + 1][:, 0:D], "xn2T_ps", g[u] + 1, "xn2T_ok")
                for u in (0, 1):
                    act.wait_ge(s["sh_ps"], g[u] + 1)
                    nc.scalar.activation(th[u][:], bank[4 * u + 3][:], ACT.Tanh, scale=0.5).then_inc(s["sh_tanh"], 1)
                for u in (0, 1):
                    copy(flat(hsT[u]), bank[4 * u + 1][:], "hsT_ps", g[u] + 1, "hsT_ok")

            attention(0, True)
            with act.Fori(1, TILES // 2 - 1) as i:
                attention(i, True)
            attention(TILES // 2 - 1, False)
            act.wait_ge(s["d_max"], 1)
            nc.scalar.activation(rt[:, 0, :], rt[:, 0, :], ACT.Exp).then_inc(s["d_exp"], 1)

            def experts(it, first=False, last=False):
                for u in range(RING):
                    j, b = RING * it + u, u % 2
                    if first and u == 0:
                        copy(xgT[0], bank[0][:, 0:D], "xgT_ps", 1, "xgT_ok")
                    if not (last and u == RING - 1):
                        copy(xgT[1 - b], bank[1 - b][:, 0:D], "xgT_ps", j + 2, "xgT_ok")
                    act.wait_ge(s["eh_ps"], j + 1)
                    nc.scalar.activation(et[b], bank[2 + b][:, 0:INTER], ACT.Tanh, scale=0.5).then_inc(s["e_tanh"], 1)
                    if not (first and u == 0):
                        result(it, u - 1)
                if last:
                    result(it, RING - 1)

            def result(it, u):
                j, b = RING * it + u, u % 2
                copy(ehT[b], bank[4 + b][:, 0:INTER], "ehT_ps", j + 1, "ehT_ok")
                n = it if u >= 0 else it - 1
                if later(n):
                    act.wait_ge(sct[u % RING], 16 * n)
                copy(ye[u % RING], bank[6 + b][:, 0:D], "y_ps", j + 1, "y_ok")

            experts(0, first=True)
            experts(1)
            with act.Fori(2, BLOCKS - 1) as it:
                experts(it)
            experts(BLOCKS - 1, last=True)
            for g in range(TILES):
                act.wait_ge(s["f_ok"], g + 1)
                act.dma_start(out[g * P:(g + 1) * P, :], fin[g % 4]).then_inc(out_s[g % 4], 16)

        @block.vector
        def _(dve):
            nc.vector.memset(kx[0][:], 0.0).then_inc(s["zeroed"], 1)
            nc.vector.memset(kx[1][:], 0.0).then_inc(s["zeroed"], 1)
            dve.wait_ge(s["ld_const"], 32)
            nc.vector.tensor_tensor(posb[:], row[:, R_POS:R_POS + D], row[:, R_B:R_B + D], ALU.add).then_inc(s["posb_ok"], 1)

            def stats(u, g, src, at, ready, tag):
                dve.wait_ge(s[ready], g + 1)
                nc.vector.bn_stats(st[u][:, at:at + 6], src).then_inc(s[tag + "_stat"], 1)
                dve.wait_ge(s["posb_ok"], 1)
                dve.wait_ge(s[tag + "_stat"], g + 1)
                nc.vector.bn_aggr(st[u][:, at + 6:at + 8], st[u][:, at:at + 6]).then_inc(s[tag + "_aggr"], 1)
                dve.wait_ge(s[tag + "_aggr"], g + 1)
                nc.vector.tensor_scalar(st[u][:, at + 8:at + 9], st[u][:, at + 7:at + 8], EPS, None,
                                        ALU.add).then_inc(s[tag + "_var"], 1)

            def normed(u, g, dst, src, at, tag, done):
                dve.wait_ge(s[tag + "_rstd"], g + 1)
                nc.vector.tensor_scalar(dst, src, st[u][:, at + 6:at + 7], st[u][:, at + 9:at + 10],
                                        ALU.subtract, ALU.mult).then_inc(s[done], 1)

            def rope(u, g, ps, cdst, sdst, ccol, scol, cok, sok):
                for dst, col, ok in ((cdst, ccol, cok), (sdst, scol, sok)):
                    nc.vector.tensor_tensor(dst[u][:].rearrange("p (h e) -> p h e", h=HEADS),
                                            ps.rearrange("p (h e) -> p h e", h=HEADS),
                                            bc(cst[:, col:col + HD], HEADS, 1), ALU.mult).then_inc(s[ok], 1)

            dve.wait_ge(s["posb_ok"], 1)

            def pair(i):
                g = [2 * i, 2 * i + 1]
                for u in (0, 1):
                    dve.wait_ge(s["emb"], g[u] + 1)
                    nc.vector.tensor_tensor(h[u][:], bank[4 * u][:, 0:D], posb[:], ALU.add).then_inc(s["h_ok"], 1)
                    stats(u, g[u], h[u][:], 0, "h_ok", "h")
                for u in (0, 1):
                    normed(u, g[u], xn[u][:], h[u][:], 0, "h", "xn_ok")
                for u in (0, 1):
                    lats = bank[4 * u + 2][:, D:D + LAT]
                    stats(u, g[u], lats, 12, "qlat", "l")
                for u in (0, 1):
                    lats = bank[4 * u + 2][:, D:D + LAT]
                    normed(u, g[u], lat[u][:], lats, 12, "l", "l_norm")
                    dve.wait_ge(s["l_norm"], g[u] + 1)
                    nc.vector.tensor_tensor(latg[u][:], lat[u][:], row[:, R_GAM:R_GAM + LAT], ALU.mult).then_inc(s["l_gam"], 1)
                    dve.wait_ge(s["l_gam"], g[u] + 1)
                    nc.vector.tensor_tensor(lat[u][:], latg[u][:], row[:, R_BET:R_BET + LAT], ALU.add).then_inc(s["lat_ok"], 1)
                for u in (0, 1):
                    rope(u, g[u], bank[4 * u + 2][:, 0:D], qc, qs, C_CQ, C_SQ, "qc_ok", "qs_ok")
                for u in (0, 1):
                    dve.wait_ge(s["k_ps"], g[u] + 1)
                    rope(u, g[u], bank[4 * u][:, 0:D], kc, ks, C_CK, C_SK, "kc_ok", "ks_ok")
                for u in (0, 1):
                    sc3 = sc[u][:].rearrange("p (h k) -> p h k", h=HEADS)
                    dve.wait_ge(s["s_ps"], g[u] + 1)
                    nc.vector.tensor_tensor(sc3, bank[4 * u + 2][:, 0:D].rearrange("p (h k) -> p h k", h=HEADS),
                                            bc(cst[:, C_CAUSAL:C_CAUSAL + T], HEADS, 1), ALU.add).then_inc(s["s_mask"], 1)
                    dve.wait_ge(s["s_mask"], g[u] + 1)
                    nc.vector.tensor_reduce(sx[u][:, 0, :], sc3, AX.X, ALU.max).then_inc(s["s_max"], 1)
                    dve.wait_ge(s["s_max"], g[u] + 1)
                    nc.vector.tensor_tensor(sc3, sc3, bc(sx[u][:, 0, :], T, 2), ALU.subtract).then_inc(s["s_sub"], 1)
                for u in (0, 1):
                    sc3 = sc[u][:].rearrange("p (h k) -> p h k", h=HEADS)
                    dve.wait_ge(s["s_exp"], g[u] + 1)
                    nc.vector.tensor_reduce(sx[u][:, 1, :], sc3, AX.X, ALU.add).then_inc(s["s_sum"], 1)
                    dve.wait_ge(s["s_sum"], g[u] + 1)
                    nc.vector.reciprocal(sx[u][:, 2, :], sx[u][:, 1, :]).then_inc(s["s_rec"], 1)
                    dve.wait_ge(s["s_rec"], g[u] + 1)
                    nc.vector.tensor_tensor(pr[u][:].rearrange("p (h k) -> p h k", h=HEADS), sc3,
                                            bc(sx[u][:, 2, :], T, 2), ALU.mult).then_inc(s["p_ok"], 1)
                for u in (0, 1):
                    dve.wait_ge(s["o_ps"], g[u] + 1)
                    nc.vector.tensor_tensor(h2[u][:], bank[4 * u][:, 0:D], h[u][:], ALU.add).then_inc(s["h2_ok"], 1)
                    stats(u, g[u], h2[u][:], 24, "h2_ok", "h2")
                for u in (0, 1):
                    if later(i):
                        dve.wait_ge(s["xn2_out"], 32 * i)
                    normed(u, g[u], xn2[u][:], h2[u][:], 24, "h2", "xn2_ok")
                for u in (0, 1):
                    dve.wait_ge(s["g_ps"], g[u] + 1)
                    nc.vector.tensor_copy(lg[:, g[u], :], bank[4 * u + 2][:, 0:E]).then_inc(s["lg_ok"], 1)
                for u in (0, 1):
                    a, b = bank[4 * u + 3], bank[4 * u]
                    dve.wait_ge(s["sh_tanh"], g[u] + 1)
                    nc.vector.scalar_tensor_tensor(hs[u][:], th[u][:], 1.0, a[:], ALU.add, ALU.mult).then_inc(s["sh_gate"], 1)
                    dve.wait_ge(s["sh_gate"], g[u] + 1)
                    nc.vector.scalar_tensor_tensor(hs[u][:], hs[u][:], 0.5, b[:], ALU.mult, ALU.mult).then_inc(s["sh_ok"], 1)
                for u in (0, 1):
                    dve.wait_ge(s["z_ps"], g[u] + 1)
                    nc.vector.tensor_tensor(acc[:, g[u], :], bank[4 * u + 2][:, 0:D], h2[u][:], ALU.add).then_inc(s["acc_ok"], 1)

            pair(0)
            with dve.Fori(1, TILES // 2) as i:
                pair(i)

            steps = [0]

            def step(ins):
                steps[0] += 1
                ins.then_inc(s["route"], 1)
                dve.wait_ge(s["route"], steps[0])

            def e3(ap):
                return ap.rearrange("p (g e) -> p g e", e=E)

            dve.wait_ge(s["lg_ok"], TILES)
            dd, pp, ss, rank, slot = (rt[:, n, :] for n in range(5))
            mx, sm, rs = (sml[:, n, :] for n in range(3))
            step(nc.vector.tensor_reduce(mx, lg[:], AX.X, ALU.max))
            nc.vector.tensor_tensor(e3(dd), lg[:], bc(mx, E, 2), ALU.subtract).then_inc(s["d_max"], 1)
            dve.wait_ge(s["d_exp"], 1)
            step(nc.vector.tensor_reduce(sm, e3(dd), AX.X, ALU.add))
            step(nc.vector.reciprocal(rs, sm))
            step(nc.vector.tensor_tensor(e3(pp), e3(dd), bc(rs, E, 2), ALU.mult))
            step(nc.vector.tensor_tensor(e3(ss), e3(pp), bc(row[:, R_BIAS:R_BIAS + E], TILES, 1), ALU.add))
            r5v = r5.rearrange("p (a f) -> p a f", f=E)
            r6v = r6.rearrange("p (a f) -> p a f", f=E)
            r5q = r5.rearrange("p (g e f) -> p g e f", e=E, f=E)
            r6q = r6.rearrange("p (g e f) -> p g e f", e=E, f=E)
            theirs, own = bc(e3(ss), E, 2), bc(e3(ss), E, 3)
            step(nc.vector.tensor_tensor(r5q, theirs, own, ALU.is_gt))
            step(nc.vector.tensor_tensor(r6q, theirs, own, ALU.is_equal))
            lt = cst[:, C_LT:C_LT + E * E]
            r6m = r6.rearrange("p (g a) -> p g a", a=E * E)
            step(nc.vector.tensor_tensor(r6m, r6m, bc(lt, TILES, 1), ALU.mult))
            step(nc.vector.tensor_tensor(r5, r5, r6, ALU.add))
            step(nc.vector.tensor_reduce(rank, r5v, AX.X, ALU.add))
            sel = rt[:, 5, :]
            for k in range(TOPK):
                step(nc.vector.tensor_scalar(isk[:, k, :], rank, float(k), None, ALU.is_equal))
            step(nc.vector.tensor_tensor(sel, isk[:, 0, :], isk[:, 1, :], ALU.add))
            dve.wait_ge(s["cnt_ps"], 1)
            cum, tot = bank[0][:, 0:G], rt[:, 6, :]
            step(nc.vector.tensor_copy(tot, bank[1][:, 0:G]))
            tot_t = tot.rearrange("p (g e) -> p e g", e=E)
            lt2 = lt.rearrange("p (a b) -> p a b", b=E)
            step(nc.vector.tensor_tensor(r5q, bc(tot_t, TILES, 1), bc(lt2, E, 2), ALU.mult))
            pre = rt[:, 7, :]
            step(nc.vector.tensor_reduce(pre, r5v, AX.X, ALU.add))
            ne, ce, off, end, off128 = (sml[:, n, :] for n in range(3, 8))
            step(nc.vector.tensor_reduce(ne, tot_t, AX.X, ALU.add))
            c64 = r6[:, 0:E * E].rearrange("p (a b) -> p a b", b=E)
            step(nc.vector.tensor_tensor(c64, bc(ne, E, 2), bc(cst[:, C_THR:C_THR + E], E, 1), ALU.is_gt))
            step(nc.vector.tensor_reduce(ce, c64, AX.X, ALU.add))
            step(nc.vector.tensor_tensor(c64, bc(ce, E, 1), lt2, ALU.mult))
            step(nc.vector.tensor_reduce(off, c64, AX.X, ALU.add))
            step(nc.vector.tensor_tensor(end, off, ce, ALU.add))
            tlv = tl[:].rearrange("p (j e) -> p j e", e=E)
            step(nc.vector.tensor_tensor(tlv, bc(end, SLOT_TILES, 1), bc(cst[:, C_TILE:C_TILE + SLOT_TILES], E, 2), ALU.is_le))
            step(nc.vector.tensor_reduce(tf[:], tlv, AX.X, ALU.add))
            nc.vector.tensor_scalar(ti[:], tf[:], float(E - 1), None, ALU.min).then_inc(s["et_ok"], 1)
            step(nc.vector.tensor_scalar(off128, off, float(P), None, ALU.mult))
            step(nc.vector.tensor_tensor(slot, cum, pre, ALU.add))
            step(nc.vector.tensor_tensor(e3(slot), e3(slot), bc(off128, TILES, 1), ALU.add))
            kkv = kk[:].rearrange("p (k a) -> p k a", k=TOPK)
            for n, of in ((0, slot), (1, pp)):
                step(nc.vector.tensor_tensor(kkv, bc(of, TOPK, 1), isk[:], ALU.mult))
                step(nc.vector.tensor_reduce(kv[:, n, :], kk[:].rearrange("p (a e) -> p a e", e=E), AX.X, ALU.add))
            dve.wait_ge(s["ld_init"], 32)
            step(nc.vector.tensor_copy(meta[:].bitcast(F32)[:, :, 2], kv[:, 1, :]))
            step(nc.vector.tensor_copy(ki[:, 0, :], kv[:, 0, :]))
            step(nc.vector.tensor_scalar(ki[:, 1, :], ki[:, 0, :], P - 1, None, ALU.bitwise_and))
            step(nc.vector.tensor_scalar(ki[:, 2, :], ki[:, 0, :], P.bit_length() - 1, None, ALU.logical_shift_right))
            nc.vector.scalar_tensor_tensor(ki[:, 3, :], ki[:, 1, :], float(SLOT_TILES), ki[:, 2, :], ALU.mult,
                                           ALU.add).then_inc(s["routed"], 1)
            dve.wait_ge(s["tab_in"], 16)
            gate = kk[:, 0:SLOT_TILES]
            step(nc.vector.tensor_scalar(gate, tb[:].bitcast(F32)[:, :, 2], 0.5, None, ALU.mult))

            def experts(it):
                for u in range(RING):
                    j, b = RING * it + u, u % 2
                    hps = bank[2 + b]
                    dve.wait_ge(s["e_tanh"], j + 1)
                    nc.vector.scalar_tensor_tensor(eh[b], et[b], 1.0, hps[:, 0:INTER], ALU.add, ALU.mult).then_inc(s["e_gate"], 1)
                    dve.wait_ge(s["e_gate"], j + 1)
                    nc.vector.scalar_tensor_tensor(eh[b], eh[b], kk[:, bass.ds(j, 1)], hps[:, INTER:2 * INTER],
                                                   ALU.mult, ALU.mult).then_inc(s["eh_ok"], 1)

            with dve.Fori(0, BLOCKS) as it:
                experts(it)
            for g in range(TILES):
                r = g % 4
                dve.wait_ge(yg_in[r], 16 * (g // 4 + 1))
                if g >= 4:
                    dve.wait_ge(out_s[r], 16 * (g // 4))
                nc.vector.tensor_tensor(fin[r], yg[r][:, 0, :], yg[r][:, 1, :], ALU.add).then_inc(s["f_add"], 1)
                dve.wait_ge(s["f_add"], g + 1)
                nc.vector.tensor_tensor(fin[r], fin[r], acc[:, g, :], ALU.add).then_inc(s["f_ok"], 1)

        @block.tensor
        def _(pe):
            def product(dst, pairs):
                for n, (a, b) in enumerate(pairs):
                    m = nc.tensor.matmul(dst, a, b, start=n == 0, stop=n == len(pairs) - 1)
                return m

            def by_image(t, hf, im):
                return t[:, hf, :, :].rearrange("p h (k i) -> p (h k) i", i=IPT)[:, :, im]

            def transposed(dst, src, blocks, ready, at, done):
                if ready:
                    pe.wait_ge(s[ready], at)
                for b in range(blocks):
                    m = nc.tensor.transpose(dst[:, b * P:(b + 1) * P], src[:, b * P:(b + 1) * P], ident)
                m.then_inc(s[done], 1)

            pe.wait_ge(s["ld_const"], 32)
            pe.wait_ge(s["ld_emb"], 16)
            pe.wait_ge(s["ld_qd"], 16)
            pe.wait_ge(s["ld_kv"], 16)
            pe.wait_ge(s["ld_o"], 32)
            pe.wait_ge(s["ld_s"], 32)

            def pair(i):
                g = [2 * i, 2 * i + 1]
                for u in (0, 1):
                    pe.wait_ge(x_in[u], 16 * (i + 1))
                    if later(i):
                        pe.wait_ge(s["acc_ok"], 2 * i)
                    product(bank[4 * u][:, 0:D], [(xt[u][:, k, :], wemb[:, k, :]) for k in range(KF)]).then_inc(s["emb"], 1)
                for u in (0, 1):
                    transposed(bank[4 * u + 1], xn[u], KD, "xn_ok", g[u] + 1, "xnT_ps")
                for u in (0, 1):
                    pe.wait_ge(s["xnT_ok"], g[u] + 1)
                    product(bank[4 * u + 2][:, 0:D + LAT], [(xnT[u][:, k, :], wqd[:, k, :]) for k in range(KD)]).then_inc(s["qlat"], 1)
                for u in (0, 1):
                    pe.wait_ge(s["ld_kv"], 16)
                    pe.wait_ge(s["lat_ok"], g[u] + 1)
                    nc.tensor.transpose(bank[4 * u + 3][0:LAT, 0:P], lat[u][:], ident).then_inc(s["latT_ps"], 1)
                for u in (0, 1):
                    pe.wait_ge(s["latT_ok"], g[u] + 1)
                    product(bank[4 * u][:, 0:D], [(latT[u][:], wkv[:, 0:D])]).then_inc(s["k_ps"], 1)
                    for hf in range(HALF):
                        m = product(bank[4 * u + 1][:, hf * P:(hf + 1) * P], [(wkv[:, D + hf * P:D + (hf + 1) * P], latT[u][:])])
                    m.then_inc(s["vT_ps"], 1)
                for u in (0, 1):
                    transposed(bank[4 * u + 3], qr[u], HALF, "qr_ok", 2 * (g[u] + 1), "qT_ps")
                for u in (0, 1):
                    pe.wait_ge(s["qs_ok"], g[u] + 1)
                    transposed(bank[4 * u + 2], kr[u], HALF, "kr_ok", 2 * (g[u] + 1), "kT_ps")
                for u in (0, 1):
                    pe.wait_ge(kx_in[u], P * (i + 1))
                    pe.wait_ge(s["qT_ok"], g[u] + 1)
                    for hf in range(HALF):
                        for im in range(IPT):
                            c = hf * P + im * T
                            m = product(bank[4 * u][:, c:c + T], [(by_image(kx[u], hf, im), qT[u][:, hf, im * T:(im + 1) * T])])
                    m.then_inc(s["sT_ps"], 1)
                for u in (0, 1):
                    pe.wait_ge(vx_in[u], P * (i + 1))
                    pe.wait_ge(s["vT_ok"], g[u] + 1)
                    for r in range(4):
                        if r >= 2:
                            pe.wait_ge(s["vx_ok"], 4 * g[u] + r - 1)
                        for q in range(4):
                            hf, im = divmod(4 * r + q, IPT)
                            m = nc.tensor.transpose(bank[4 * u + 1 + 2 * (r % 2)][:, q * P:(q + 1) * P],
                                                    by_image(vxT[u], hf, im), ident)
                        m.then_inc(s["vx_ps"], 1)
                    transposed(bank[4 * u + 2], sT[u][:].rearrange("p a b -> p (a b)"), HALF, "sT_ok", g[u] + 1, "s_ps")
                for u in (0, 1):
                    transposed(bank[4 * u], pr[u], HALF, "p_ok", g[u] + 1, "pT_ps")
                for u in (0, 1):
                    pe.wait_ge(s["pT_ok"], g[u] + 1)
                    pe.wait_ge(s["vx_ok"], 4 * g[u] + 4)
                    for hf in range(HALF):
                        for im in range(IPT):
                            c = hf * P + im * T
                            m = product(bank[4 * u + 2][:, c:c + T], [(vx[u][:, hf * IPT + im, :], pT[u][:, hf, im * T:(im + 1) * T])])
                    m.then_inc(s["oT_ps"], 1)
                for u in (0, 1):
                    pe.wait_ge(s["oT_ok"], g[u] + 1)
                    product(bank[4 * u][:, 0:D], [(oT[u][:, k, :], wo[:, k, :]) for k in range(KD)]).then_inc(s["o_ps"], 1)
                for u in (0, 1):
                    transposed(bank[4 * u + 1], xn2[u], KD, "xn2_ok", g[u] + 1, "xn2T_ps")
                for u in (0, 1):
                    pe.wait_ge(s["xn2T_ok"], g[u] + 1)
                    product(bank[4 * u + 2][:, 0:E], [(xn2T[u][:, k, :], wg[:, k, :]) for k in range(KD)]).then_inc(s["g_ps"], 1)
                    product(bank[4 * u + 3][:], [(xn2T[u][:, k, :], ws13[:, k, 0:SINTER]) for k in range(KD)])
                    product(bank[4 * u][:], [(xn2T[u][:, k, :], ws13[:, k, SINTER:]) for k in range(KD)]).then_inc(s["sh_ps"], 1)
                for u in (0, 1):
                    transposed(bank[4 * u + 1], hs[u], KS, "sh_ok", g[u] + 1, "hsT_ps")
                for u in (0, 1):
                    pe.wait_ge(s["hsT_ok"], g[u] + 1)
                    pe.wait_ge(s["lg_ok"], g[u] + 1)
                    product(bank[4 * u + 2][:, 0:D], [(hsT[u][:, k, :], ws2[:, k, :]) for k in range(KS)]).then_inc(s["z_ps"], 1)

            pair(0)
            with pe.Fori(1, TILES // 2) as i:
                pair(i)

            pe.wait_ge(s["acc_ok"], TILES)
            pe.wait_ge(s["route"], 13)
            product(bank[0][:, 0:TILES * E], [(cst[:, C_TRI:C_TRI + P], rt[:, 5, :])])
            product(bank[1][:, 0:TILES * E], [(cst[:, C_ONE:C_ONE + P], rt[:, 5, :])]).then_inc(s["cnt_ps"], 1)

            pe.wait_ge(s["ld_e"], 32 * E)
            pe.wait_ge(s["et_ok"], 1)
            pe.wait_ge(s["routed"], 1)

            def gathered(it, u):
                j = RING * it + u
                r, b = u % RING, u % 2
                pe.wait_ge(gat[r], 16 * (it + 1 + u // RING))
                if later(j):
                    pe.wait_ge(s["xgT_ok"], j)
                transposed(bank[b], xg[r], KD, None, 0, "xgT_ps")

            def up(it, u, load):
                j, b = RING * it + u, u % 2
                pe.wait_ge(s["xgT_ok"], j + 1)
                product(bank[2 + b][:], [(xgT[b][:, k * P:(k + 1) * P], load[:, k * 2 * INTER:(k + 1) * 2 * INTER]) for k in range(KD)])\
                    .then_inc(s["eh_ps"], 1)

            def down(it, u, w):
                j, b = RING * it + u, u % 2
                transposed(bank[4 + b], eh[b], KI, "eh_ok", j + 1, "ehT_ps")
                pe.wait_ge(s["ehT_ok"], j + 1)
                product(bank[6 + b][:, 0:D], [(ehT[b][:, k * P:(k + 1) * P], w[:, k * D:(k + 1) * D]) for k in range(KI)])\
                    .then_inc(s["y_ps"], 1)

            def expert(it, u):
                j = RING * it + u
                at = ti[0:1, j:j + 1] if isinstance(j, int) else ti[0:1, bass.ds(j, 1)]
                return pe.value_load(at, min_val=0, max_val=E - 1)

            def experts(it, first=False, last=False):
                for u in range(RING):
                    if first and u == 0:
                        gathered(it, 0)
                    if not (last and u == RING - 1):
                        gathered(it, u + 1)
                    e = expert(it, u)
                    up(it, u, we13[:, e, :])
                    if not (first and u == 0):
                        d = expert(it, u - 1)
                        down(it, u - 1, we2[:, d, :])
                if last:
                    down(it, RING - 1, we2[:, expert(it, RING - 1), :])

            experts(0, first=True)
            with pe.Fori(1, BLOCKS - 1) as it:
                experts(it)
            experts(BLOCKS - 1, last=True)


def constants():
    c = np.zeros((P, C_END), np.float32)
    p = np.arange(P)
    c[:, C_ID:C_ID + P] = np.eye(P)
    c[:, C_TRI:C_TRI + P] = p[:, None] < p[None, :]
    c[:, C_ONE:C_ONE + P] = 1.0
    half = HD // 2
    inv = (1.0 / np.float32(10000.0) ** (np.arange(half, dtype=np.float32) / np.float32(half))).astype(np.float32)
    ang = (p % T).astype(np.float32)[:, None] * inv[None, :]
    cos, sin = np.cos(ang), np.sin(ang)
    both = np.concatenate([cos, cos], 1)
    cross = np.concatenate([sin, -sin], 1)
    scale = 1.0 / np.sqrt(HD)
    c[:, C_CQ:C_CQ + HD], c[:, C_SQ:C_SQ + HD] = both * scale, cross * scale
    c[:, C_CK:C_CK + HD], c[:, C_SK:C_SK + HD] = both, cross
    c[:, C_CAUSAL:C_CAUSAL + T] = np.where(np.arange(T)[None, :] <= (p % T)[:, None], 0.0, -3.0e38)
    e = np.arange(E)
    c[:, C_LT:C_LT + E * E] = (e[None, :] < e[:, None]).reshape(-1)
    c[:, C_THR:C_THR + E] = P * e
    c[:, C_TILE:C_TILE + SLOT_TILES] = np.arange(SLOT_TILES)
    c[:, C_MHALF] = -0.5
    meta = np.zeros((P, TOPK, TILES, 4), np.int32)
    token = np.arange(TILES)[None, :] * P + p[:, None]
    for k in range(TOPK):
        meta[:, k, :, 0] = token
        meta[:, k, :, 1] = token * TOPK + k
    table = np.zeros((P, SLOT_TILES, 4), np.int32)
    table[:, :, 1] = TOKENS * TOPK + p[:, None] + P * np.arange(SLOT_TILES)[None, :]
    return c, meta.reshape(P, -1), table.reshape(P * SLOT_TILES, 4)


def kernel(x, L0_tok_W, L0_tok_b, L0_tok_pos_emb, L0_attn_W_q, L0_attn_W_dkv, L0_attn_W_uk, L0_attn_W_uv, L0_attn_W_o,
           L0_attn_ln_gamma, L0_attn_ln_beta, L0_ffn_gate_w, L0_ffn_gate_bias, L0_ffn_w1, L0_ffn_w3, L0_ffn_w2,
           L0_ffn_sw1, L0_ffn_sw3, L0_ffn_sw2):
    import concourse.bacc as bacc
    from concourse.bass_utils import run_bass_kernel_spmd

    a = np.asarray

    def blocks(w, k):
        w = a(w)
        return np.ascontiguousarray(w.reshape(k, P, -1).transpose(1, 0, 2).reshape(P, -1))

    def spread(v):
        return np.broadcast_to(a(v)[None, :], (P, a(v).shape[0]))

    xs = a(x).reshape(TILES, IPT, CH, NP, PS, NP, PS).transpose(0, 2, 4, 6, 1, 3, 5).reshape(TILES, KF, P, P)
    c, meta, table = constants()
    ins = {
        "xp": np.ascontiguousarray(xs.transpose(0, 2, 1, 3).reshape(TILES, P, KF * P)),
        "w_emb": blocks(a(L0_tok_W).T, KF),
        "w_qd": blocks(np.concatenate([a(L0_attn_W_q), a(L0_attn_W_dkv)], 1), KD),
        "w_kv": np.ascontiguousarray(np.concatenate([a(L0_attn_W_uk), a(L0_attn_W_uv)], 1)),
        "w_o": blocks(L0_attn_W_o, KD),
        "w_gate": blocks(a(L0_ffn_gate_w).T, KD),
        "w_s13": blocks(np.concatenate([a(L0_ffn_sw1).T, a(L0_ffn_sw3).T], 1), KD),
        "w_s2": blocks(a(L0_ffn_sw2).T, KS),
        "w_e13": np.stack([blocks(np.concatenate([a(L0_ffn_w1)[e].T, a(L0_ffn_w3)[e].T], 1), KD) for e in range(E)]),
        "w_e2": np.stack([blocks(a(L0_ffn_w2)[e].T, KI) for e in range(E)]),
        "rows": np.ascontiguousarray(np.concatenate(
            [np.tile(a(L0_tok_pos_emb), (IPT, 1)), spread(L0_tok_b), spread(L0_attn_ln_gamma), spread(L0_attn_ln_beta),
             spread(L0_ffn_gate_bias)], 1)),
        "consts": c, "meta0": meta, "table0": table,
    }
    nc = bacc.Bacc("TRN2", target_bir_lowering=False, num_devices=1)
    args = [nc.dram_tensor(n, v.shape, mybir.dt.from_np(v.dtype), kind="ExternalInput").ap() for n, v in ins.items()]
    args.append(nc.dram_tensor("out", (TOKENS, D), F32, kind="ExternalOutput").ap())
    build(nc, *args)
    r = run_bass_kernel_spmd(nc, [ins], core_ids=[0])
    return r.results[0]["out"].reshape(IMAGES, T, D)
```

```python
from contextlib import ExitStack

import numpy as np

import concourse.bass as bass
from concourse import mybir

F32 = mybir.dt.float32
I32 = mybir.dt.int32
ALU = mybir.AluOpType
ACT = mybir.ActivationFunctionType
AX = mybir.AxisListType

P = 128
IMAGES, CH, IMG, PS = 64, 3, 64, 16
NP = IMG // PS
T = NP * NP
D = 256
KD = D // P
FEAT = CH * PS * PS
KF = FEAT // P
HEADS, HD = 16, 16
HALF = 2
HPH = HEADS // HALF
LAT = 64
TOKENS = IMAGES * T
TILES = TOKENS // P
IPT = P // T
QG = 32
IPG = P // QG
GROUPS = IPT // IPG
E, INTER, TOPK = 8, 256, 2
KI = INTER // P
SINTER = 2 * INTER
KS = SINTER // P
SLOT_TILES = TOKENS * TOPK // P + E
EPS = 1e-5
RING = 4
BLOCKS = SLOT_TILES // RING

C_ID = 0
C_TRI = C_ID + P
C_ONE = C_TRI + P
C_CQ = C_ONE + P
C_SQ = C_CQ + HD
C_CK = C_SQ + HD
C_SK = C_CK + HD
C_CAUSAL = C_SK + HD
C_LT = C_CAUSAL + T
C_THR = C_LT + E * E
C_TILE = C_THR + E
C_MHALF = C_TILE + SLOT_TILES
C_HEAD = C_MHALF + 1
C_END = C_HEAD + HPH
R_POS = 0
R_B = R_POS + D
R_GAM = R_B + D
R_BET = R_GAM + LAT
R_BIAS = R_BET + LAT
R_END = R_BIAS + E


def bc(ap, n, at):
    pairs = [list(x) for x in ap.ap]
    shape = list(ap.shape)
    out = ap.unsqueeze(at)
    shape.insert(at, n)
    return out.broadcast_to(shape)


def later(i):
    return not isinstance(i, int) or i > 0


def build(nc, xp, w_emb, w_qd, w_kv, w_o, w_gs, w_s2, w_e13, w_e2, rows, consts, meta0, table0, out):
    ctx = ExitStack()
    with ctx:
        def sb(name, shape, dt=F32):
            return ctx.enter_context(nc.sbuf_tensor(name, shape, dt))

        def sem(name):
            return ctx.enter_context(nc.semaphore(name))

        bank = [ctx.enter_context(nc.psum_tensor(f"bank{i}", [P, 512], F32)) for i in range(8)]
        pj = [bank[0:2], bank[2:4]]
        at = [bank[4:6], bank[6:8]]

        xn_rows = nc.dram_tensor("xn_rows", (TOKENS, D), F32).ap()
        table = nc.dram_tensor("slot_table", (P * SLOT_TILES, 4), I32).ap()
        y_rows = nc.dram_tensor("y_rows", (TOKENS * TOPK + P * SLOT_TILES, D), F32).ap()

        wemb = sb("wemb", [P, KF, D])
        wqd = sb("wqd", [P, KD, D + LAT])
        wkv = sb("wkv", [LAT, 2 * D])
        wo = sb("wo", [P, KD, D])
        wgs = sb("wgs", [P, KD, E + 2 * SINTER])
        ws2 = sb("ws2", [P, KS, D])
        we13 = sb("we13", [P, E, KD * 2 * INTER])
        we2 = sb("we2", [P, E, KI * D])
        cst = sb("cst", [P, C_END])
        row = sb("row", [P, R_END])
        ident = cst[:, C_ID:C_ID + P]
        xt = [sb(f"xt{u}", [P, KF, P]) for u in (0, 1)]
        posb = sb("posb", [P, D])
        st = [sb(f"st{u}", [P, 40]) for u in (0, 1)]
        xn = [sb(f"xn{u}", [P, D]) for u in (0, 1)]
        xnT = [sb(f"xnT{u}", [P, KD * P]) for u in (0, 1)]
        qc = [sb(f"qc{u}", [P, D]) for u in (0, 1)]
        qs = [sb(f"qs{u}", [P, D]) for u in (0, 1)]
        qr = [sb(f"qr{u}", [P, D]) for u in (0, 1)]
        kc = [sb(f"kc{u}", [P, D]) for u in (0, 1)]
        ks = [sb(f"ks{u}", [P, D]) for u in (0, 1)]
        kr = [sb(f"kr{u}", [P, D]) for u in (0, 1)]
        lat = [sb(f"lat{u}", [P, LAT]) for u in (0, 1)]
        latg = [sb(f"latg{u}", [P, LAT]) for u in (0, 1)]
        latT = [sb(f"latT{u}", [LAT, P]) for u in (0, 1)]
        qT = [sb(f"qT{u}", [P, HALF * P + QG - T]) for u in (0, 1)]
        pT = [sb(f"pT{u}", [P, GROUPS * HALF * P]) for u in (0, 1)]
        kx = [sb(f"kx{u}", [P, HALF * IPT, HPH, T]) for u in (0, 1)]
        vxT = [sb(f"vxT{u}", [P, HALF * IPT, HPH, T]) for u in (0, 1)]
        vx = [sb(f"vx{u}", [P, HALF * IPT, P]) for u in (0, 1)]
        sc = [sb(f"sc{u}", [P, GROUPS * D]) for u in (0, 1)]
        on = [sb(f"on{u}", [P, GROUPS * D]) for u in (0, 1)]
        sx = [sb(f"sx{u}", [P, 3, GROUPS * HEADS]) for u in (0, 1)]
        oT = [sb(f"oT{u}", [P, KD * P]) for u in (0, 1)]
        xn2 = [sb(f"xn2{u}", [P, D]) for u in (0, 1)]
        gxT = [sb(f"gxT{u}", [P, KD * P]) for u in (0, 1)]
        xn2T = sb("xn2T", [P, TILES, KD * P])
        acc = sb("acc", [P, TILES, D])
        th = [sb(f"th{u}", [P, SINTER]) for u in (0, 1)]
        hs = [sb(f"hs{u}", [P, SINTER]) for u in (0, 1)]
        hsT = [sb(f"hsT{u}", [P, KS * P]) for u in (0, 1)]
        lg = sb("lg", [P, TILES, E])
        G = TILES * E
        rt = sb("rt", [P, 8, G])
        r5 = vx[1][:, 0:4, :].rearrange("p a b -> p (a b)")
        r6 = vx[1][:, 4:8, :].rearrange("p a b -> p (a b)")
        isk = sb("isk", [P, TOPK, G])
        sml = sb("sml", [P, 8, E])
        kk = sb("kk", [P, TOPK * G])
        kv = sb("kv", [P, 2, TOPK * TILES])
        ki = sb("ki", [P, 4, TOPK * TILES], I32)
        tl = sb("tl", [P, SLOT_TILES * E])
        tf = sb("tf", [P, SLOT_TILES])
        ti = sb("ti", [P, SLOT_TILES], I32)
        meta = sb("meta", [P, TOPK * TILES, 4], I32)
        tb = sb("tb", [P, SLOT_TILES, 4], I32)

        def part(t, r, n):
            flat = t[:].rearrange("p a b c -> p (a b c)") if len(t.shape) == 4 else t[:].rearrange("p a b -> p (a b)")
            return flat[:, r * n:(r + 1) * n]

        xg = [part(vxT[0], r, D) for r in range(RING)]
        ye = [part(vxT[1], r, D) for r in range(RING)]
        xgT, et, eh, ehT = ([part(vx[0], 2 * n + r, D) for r in (0, 1)] for n in range(4))
        yg = [part(kx[r // 2], r % 2, 2 * TOPK * D).rearrange("p (g k d) -> p g k d", g=2, k=TOPK) for r in range(TILES // 2)]

        names = """ld_const ld_emb ld_qd ld_kv ld_o ld_s ld_e ld_init x_in0 x_in1 padded posb_ok
            emb h_ok h_stat h_aggr h_var h_rstd xn_ok xnT_ps xnT_ok qlat
            qc_ok qs_ok qr_ok l_stat l_aggr l_var l_rstd l_norm l_gam lat_ok latT_ps latT_ok qT_ps qT_ok
            k_ps kc_ok ks_ok kr_ok vT_ps vT_ok kT_ps kx_ok vx_ps vx_ok
            s_ps s_mask s_max s_sub s_exp s_sum s_rec pT_ps pT_ok pv_ps on_ok oT_ps oT_ok o_ps h2_ok
            h2_stat h2_aggr h2_var h2_rstd xn2_ok xn2T_ps xn2T_ok xn2T_kept xn2_out g_ps lg_ok
            sh_ps sh_tanh sh_gate sh_ok hsT_ps hsT_ok z_ps acc_ok
            route d_max d_exp cnt_ps routed scattered tab_in et_ok
            gat0 gat1 gat2 gat3 xgT_ps xgT_ok eh_ps e_tanh e_gate eh_ok ehT_ps ehT_ok y_ps y_ok
            sct0 sct1 sct2 sct3 yg0 yg1 yg2 yg3 f_add f_ok out_a out_b""".split()
        s = {n: sem(n) for n in names}
        x_in = (s["x_in0"], s["x_in1"])
        gat = [s[f"gat{r}"] for r in range(RING)]
        sct = [s[f"sct{r}"] for r in range(RING)]
        yg_in = [s[f"yg{r}"] for r in range(4)]
        PAIRS = TILES // 2
        steps_of = {"d": 0}

        block = ctx.enter_context(nc.Block())

        def heads(ap):
            return ap.rearrange("p (h j d) -> p h j d", h=HEADS, j=2)

        def by_head(ap):
            return ap.rearrange("p (h e) -> p h e", e=HD)

        @block.sync
        def _(sp):
            sp.dma_start(xt[0][:], xp[0]).then_inc(x_in[0], 16)
            sp.dma_start(cst[:], consts).then_inc(s["ld_const"], 16)
            sp.dma_start(row[:], rows).then_inc(s["ld_const"], 16)
            sp.dma_start(wqd[:], w_qd).then_inc(s["ld_qd"], 16)
            sp.dma_start(wkv[:], w_kv).then_inc(s["ld_kv"], 16)

            def patches(g, u):
                sp.wait_ge(s["emb"], g + 1)
                sp.dma_start(xt[u][:], xp[g + 2]).then_inc(x_in[u], 16)

            def rows_out(g, u):
                sp.wait_ge(s["xn2_ok"], g + 1)
                sp.dma_start(xn_rows[bass.ds(g * P, P), :], xn2[u][:]).then_inc(s["xn2_out"], 16)

            for u in (0, 1):
                patches(u, u)
            sp.dma_start(wo[:], w_o).then_inc(s["ld_o"], 16)
            sp.dma_start(wgs[:], w_gs).then_inc(s["ld_s"], 16)
            sp.dma_start(ws2[:], w_s2).then_inc(s["ld_s"], 16)
            sp.dma_start(table, table0).then_inc(s["ld_init"], 16)
            sp.dma_start(meta[:], meta0).then_inc(s["ld_init"], 16)
            for i in range(PAIRS):
                for u in (0, 1):
                    if i < PAIRS - 2:
                        patches(2 * i + 2 + u, u)
                for u in (0, 1):
                    rows_out(2 * i + u, u)
            sp.wait_ge(s["scattered"], 16 * TOPK * TILES)
            sp.dma_start(tb[:], table.rearrange("(p j) c -> p j c", p=P)).then_inc(s["tab_in"], 16)
            for r in range(RING):
                sp.wait_ge(sct[r], 16 * BLOCKS)
            y_tok = y_rows[0:TOKENS * TOPK, :].rearrange("(g p k) d -> p g k d", p=P, k=TOPK)
            for r in range(4):
                sp.dma_start(yg[r], y_tok[:, 2 * r:2 * r + 2]).then_inc(yg_in[r], 16)
            for g in range(0, TILES, 2):
                sp.wait_ge(s["f_ok"], g // 2 + 1)
                sp.dma_start(out[g * P:(g + 1) * P, :], acc[:, g, :]).then_inc(s["out_a"], 16)
            sp.wait_ge(s["out_a"], 16 * PAIRS)
            sp.wait_ge(s["out_b"], 16 * PAIRS)

        @block.gpsimd
        def _(pool):
            for u in (0, 1):
                nc.gpsimd.memset(qT[u][:, HALF * P:], 0.0).then_inc(s["padded"], 1)

            def rstd(u, g, src, tag):
                pool.wait_ge(s[tag + "_var"], g + 1)
                nc.gpsimd.tensor_tensor(st[u][:, src + 1:src + 2], st[u][:, src:src + 1], cst[:, C_MHALF:C_MHALF + 1],
                                        ALU.pow).then_inc(s[tag + "_rstd"], 1)

            def body(i, proj=True, attn=True):
                b = [2 * i, 2 * i + 1]
                a = [2 * i + 2, 2 * i + 3]
                if proj:
                    rstd(0, a[0], 8, "h")
                    rstd(1, a[1], 8, "h")
                    rstd(0, a[0], 20, "l")
                    rstd(1, a[1], 20, "l")
                if attn:
                    rstd(0, b[0], 32, "h2")
                    rstd(1, b[1], 32, "h2")

            pool.wait_ge(s["ld_const"], 32)
            body(-1, attn=False)
            body(0)
            with pool.Fori(1, PAIRS - 1) as i:
                body(i)
            body(PAIRS - 1, proj=False)
            pool.wait_ge(s["routed"], 1)
            pool.wait_ge(s["ld_init"], 32)
            for c in range(TOPK * TILES):
                nc.gpsimd.indirect_dma_start(
                    out=table, out_offset=bass.IndirectOffsetOnAxis(ap=ki[:, 3, c:c + 1], axis=0),
                    in_=meta[:, c, :], in_offset=None).then_inc(s["scattered"], 16)
            pool.wait_ge(s["tab_in"], 16)
            pool.wait_ge(s["xn2_out"], 16 * TILES)

            def gather(j):
                nc.gpsimd.indirect_dma_start(
                    out=xg[j % RING], out_offset=None, in_=xn_rows,
                    in_offset=bass.IndirectOffsetOnAxis(ap=tb[:, j, 0:1], axis=0)).then_inc(gat[j % RING], 16)

            def scatter(j):
                pool.wait_ge(s["y_ok"], j + 1)
                nc.gpsimd.indirect_dma_start(
                    out=y_rows, out_offset=bass.IndirectOffsetOnAxis(ap=tb[:, j, 1:2], axis=0),
                    in_=ye[j % RING], in_offset=None).then_inc(sct[j % RING], 16)

            for j in range(RING):
                gather(j)
            for j in range(SLOT_TILES):
                if j + RING < SLOT_TILES:
                    pool.wait_ge(s["xgT_ps"], j + 1)
                    gather(j + RING)
                if j > 0:
                    scatter(j - 1)
            scatter(SLOT_TILES - 1)

        @block.scalar
        def _(act):
            act.dma_start(wemb[:], w_emb).then_inc(s["ld_emb"], 16)
            act.dma_start(xt[1][:], xp[1]).then_inc(x_in[1], 16)

            def copy(dst, src, ready, at, done):
                act.wait_ge(s[ready], at)
                nc.scalar.copy(dst, src).then_inc(s[done], 1)

            def v_blocks(u, g):
                act.wait_ge(s["padded"], 2)
                act.wait_ge(s["vT_ps"], g + 1)
                for hd in range(HPH):
                    m = nc.scalar.activation(vxT[u][:, :, hd, :], pj[u][0][:, 0:D].rearrange("p (a k) -> p a k", k=T),
                                             ACT.Copy, scale=cst[:, C_HEAD + hd:C_HEAD + hd + 1])
                m.then_inc(s["vT_ok"], 1)

            def vx_round(u, g, r):
                copy(vx[u][:, 4 * r:4 * r + 4, :].rearrange("p a b -> p (a b)"), pj[u][1 - r % 2][:],
                     "vx_ps", 4 * g + r + 1, "vx_ok")

            def exp(u, g):
                act.wait_ge(s["s_sub"], g + 1)
                nc.scalar.activation(sc[u][:], sc[u][:], ACT.Exp).then_inc(s["s_exp"], 1)

            def pT_copy(u, g):
                copy(pT[u][:], at[u][1][:], "pT_ps", g + 1, "pT_ok")

            def oT_copy(u, g):
                copy(oT[u][:].rearrange("p (i q) -> p i q", q=T), at[u][1][:].rearrange("p (i q) -> p i q", q=QG)[:, :, 0:T],
                     "oT_ps", g + 1, "oT_ok")

            def body(i, proj=True, attn=True, extra=None):
                b = [2 * i, 2 * i + 1]
                a = [2 * i + 2, 2 * i + 3]
                if attn:
                    exp(0, b[0])
                if proj:
                    copy(xnT[0][:], pj[0][1][:, 0:D], "xnT_ps", a[0] + 1, "xnT_ok")
                if attn:
                    pT_copy(0, b[0])
                    exp(1, b[1])
                if proj:
                    copy(xnT[1][:], pj[1][1][:, 0:D], "xnT_ps", a[1] + 1, "xnT_ok")
                if attn:
                    pT_copy(1, b[1])
                if proj:
                    copy(latT[0][:], pj[0][1][0:LAT, 0:P], "latT_ps", a[0] + 1, "latT_ok")
                if attn:
                    oT_copy(0, b[0])
                if proj:
                    copy(latT[1][:], pj[1][1][0:LAT, 0:P], "latT_ps", a[1] + 1, "latT_ok")
                    v_blocks(0, a[0])
                if attn:
                    oT_copy(1, b[1])
                    copy(gxT[0][:], at[0][1][:, 0:D], "xn2T_ps", b[0] + 1, "xn2T_ok")
                    nc.scalar.copy(xn2T[:, b[0], :], at[0][1][:, 0:D]).then_inc(s["xn2T_kept"], 1)
                if proj:
                    copy(qT[0][:, 0:D], pj[0][1][:, 0:D], "qT_ps", a[0] + 1, "qT_ok")
                    v_blocks(1, a[1])
                    for r in range(4):
                        vx_round(0, a[0], r)
                if attn:
                    copy(gxT[1][:], at[1][1][:, 0:D], "xn2T_ps", b[1] + 1, "xn2T_ok")
                    nc.scalar.copy(xn2T[:, b[1], :], at[1][1][:, 0:D]).then_inc(s["xn2T_kept"], 1)
                if proj:
                    copy(qT[1][:, 0:D], pj[1][1][:, 0:D], "qT_ps", a[1] + 1, "qT_ok")
                    for r in range(4):
                        vx_round(1, a[1], r)

            body(-1, attn=False)
            for e in range(E):
                act.dma_start(we13[:, e, :], w_e13[e]).then_inc(s["ld_e"], 16)
                act.dma_start(we2[:, e, :], w_e2[e]).then_inc(s["ld_e"], 16)
            body(0)
            with act.Fori(1, PAIRS - 1) as i:
                body(i)
            body(PAIRS - 1, proj=False)

            def shared(g):
                u = g % 2
                act.wait_ge(s["sh_ps"], g + 1)
                nc.scalar.activation(th[u][:], bank[2 * u][:], ACT.Tanh, scale=0.5).then_inc(s["sh_tanh"], 1)

            def shared_T(g):
                copy(hsT[g % 2][:], bank[4 + g % 2][:], "hsT_ps", g + 1, "hsT_ok")

            act.wait_ge(s["d_max"], 1)
            nc.scalar.activation(rt[:, 0, :], rt[:, 0, :], ACT.Exp).then_inc(s["d_exp"], 1)
            shared(0)
            for g in range(1, TILES):
                shared(g)
                shared_T(g - 1)
            shared_T(TILES - 1)

            def experts(it, first=False, last=False):
                for u in range(RING):
                    j, b = RING * it + u, u % 2
                    if first and u == 0:
                        copy(xgT[0], bank[0][:, 0:D], "xgT_ps", 1, "xgT_ok")
                        copy(xgT[1], bank[1][:, 0:D], "xgT_ps", 2, "xgT_ok")
                        tanh(0, 0)
                    if not (last and u == RING - 1):
                        tanh(j + 1, 1 - b)
                    if not (last and u >= RING - 2):
                        copy(xgT[b], bank[b][:, 0:D], "xgT_ps", j + 3, "xgT_ok")
                    copy(ehT[b], bank[4 + b][:, 0:INTER], "ehT_ps", j + 1, "ehT_ok")
                    if not (first and u == 0):
                        result(it, u - 1)
                if last:
                    result(it, RING - 1)

            def tanh(j, b):
                act.wait_ge(s["eh_ps"], j + 1)
                nc.scalar.activation(et[b], bank[2 + b][:, 0:INTER], ACT.Tanh, scale=0.5).then_inc(s["e_tanh"], 1)

            def result(it, u):
                j, b = RING * it + u, u % 2
                n = it if u >= 0 else it - 1
                if later(n):
                    act.wait_ge(sct[u % RING], 16 * n)
                copy(ye[u % RING], bank[6 + b][:, 0:D], "y_ps", j + 1, "y_ok")

            experts(0, first=True)
            experts(1)
            with act.Fori(2, BLOCKS - 1) as it:
                experts(it)
            experts(BLOCKS - 1, last=True)
            for g in range(1, TILES, 2):
                act.wait_ge(s["f_ok"], g // 2 + 1)
                act.dma_start(out[g * P:(g + 1) * P, :], acc[:, g, :]).then_inc(s["out_b"], 16)

        @block.vector
        def _(dve):
            dve.wait_ge(s["ld_const"], 32)
            nc.vector.tensor_tensor(posb[:], row[:, R_POS:R_POS + D], row[:, R_B:R_B + D], ALU.add).then_inc(s["posb_ok"], 1)

            def stats(u, g, src, col, ready, tag):
                dve.wait_ge(s["posb_ok"], 1)
                dve.wait_ge(s[ready], g + 1)
                nc.vector.bn_stats(st[u][:, col:col + 6], src).then_inc(s[tag + "_stat"], 1)
                dve.wait_ge(s["posb_ok"], 1)
                dve.wait_ge(s[tag + "_stat"], g + 1)
                nc.vector.bn_aggr(st[u][:, col + 6:col + 8], st[u][:, col:col + 6]).then_inc(s[tag + "_aggr"], 1)
                dve.wait_ge(s[tag + "_aggr"], g + 1)
                nc.vector.tensor_scalar(st[u][:, col + 8:col + 9], st[u][:, col + 7:col + 8], EPS, None,
                                        ALU.add).then_inc(s[tag + "_var"], 1)

            def normed(u, g, dst, src, col, tag, done):
                dve.wait_ge(s[tag + "_rstd"], g + 1)
                nc.vector.tensor_scalar(dst, src, st[u][:, col + 6:col + 7], st[u][:, col + 9:col + 10],
                                        ALU.subtract, ALU.mult).then_inc(s[done], 1)

            def embedded(u, g):
                dve.wait_ge(s["emb"], g + 1)
                nc.vector.tensor_tensor(acc[:, g, :], pj[u][0][:, 0:D], posb[:], ALU.add).then_inc(s["h_ok"], 1)
                stats(u, g, acc[:, g, :], 0, "h_ok", "h")

            def latent(u, g):
                normed(u, g, lat[u][:], pj[u][0][:, D:D + LAT], 12, "l", "l_norm")
                dve.wait_ge(s["l_norm"], g + 1)
                nc.vector.tensor_tensor(latg[u][:], lat[u][:], row[:, R_GAM:R_GAM + LAT], ALU.mult).then_inc(s["l_gam"], 1)
                dve.wait_ge(s["l_gam"], g + 1)
                nc.vector.tensor_tensor(lat[u][:], latg[u][:], row[:, R_BET:R_BET + LAT], ALU.add).then_inc(s["lat_ok"], 1)

            def rope(u, g, ps, c, sn, r, ccol, scol, tag):
                for dst, col, ok in ((c, ccol, tag + "c_ok"), (sn, scol, tag + "s_ok")):
                    nc.vector.tensor_tensor(dst[u][:].rearrange("p (h e) -> p h e", h=HEADS),
                                            ps.rearrange("p (h e) -> p h e", h=HEADS),
                                            bc(cst[:, col:col + HD], HEADS, 1), ALU.mult).then_inc(s[ok], 1)
                dve.wait_ge(s[tag + "s_ok"], g + 1)
                for j in (0, 1):
                    nc.vector.tensor_tensor(heads(r[u][:])[:, :, j, :], heads(c[u][:])[:, :, j, :],
                                            heads(sn[u][:])[:, :, 1 - j, :], ALU.add).then_inc(s[tag + "r_ok"], 1)

            def rope_q(u, g):
                rope(u, g, pj[u][0][:, 0:D], qc, qs, qr, C_CQ, C_SQ, "q")

            def rope_k(u, g):
                dve.wait_ge(s["k_ps"], g + 1)
                rope(u, g, pj[u][1][:, 0:D], kc, ks, kr, C_CK, C_SK, "k")

            def k_blocks(u, g):
                dve.wait_ge(s["kT_ps"], g + 1)
                for hf in range(HALF):
                    kT = pj[u][0][:, hf * P:(hf + 1) * P].rearrange("p (i k) -> p i k", k=T)
                    of = bc(bc(cst[:, C_HEAD:C_HEAD + HPH], T, 2), IPT, 1)
                    nc.vector.tensor_tensor(kx[u][:, hf * IPT:(hf + 1) * IPT], bc(kT, HPH, 2), of,
                                            ALU.mult).then_inc(s["kx_ok"], 1)

            def softmax1(u, g):
                sc3, mx = by_head(sc[u][:]), sx[u][:, 0, :]
                dve.wait_ge(s["s_ps"], g + 1)
                nc.vector.tensor_tensor(sc3, by_head(at[u][0][:]), bc(cst[:, C_CAUSAL:C_CAUSAL + T], GROUPS * HEADS, 1),
                                        ALU.add).then_inc(s["s_mask"], 1)
                dve.wait_ge(s["s_mask"], g + 1)
                nc.vector.tensor_reduce(mx, sc3, AX.X, ALU.max).then_inc(s["s_max"], 1)
                dve.wait_ge(s["s_max"], g + 1)
                nc.vector.tensor_tensor(sc3, sc3, bc(mx, T, 2), ALU.subtract).then_inc(s["s_sub"], 1)

            def softmax2(u, g):
                dve.wait_ge(s["s_exp"], g + 1)
                nc.vector.tensor_reduce(sx[u][:, 1, :], by_head(sc[u][:]), AX.X, ALU.add).then_inc(s["s_sum"], 1)
                dve.wait_ge(s["s_sum"], g + 1)
                nc.vector.reciprocal(sx[u][:, 2, :], sx[u][:, 1, :]).then_inc(s["s_rec"], 1)

            def attended(u, g):
                dve.wait_ge(s["s_rec"], g + 1)
                dve.wait_ge(s["pv_ps"], g + 1)
                nc.vector.tensor_tensor(by_head(on[u][:]), by_head(at[u][0][:]), bc(sx[u][:, 2, :], HD, 2), ALU.mult)\
                    .then_inc(s["on_ok"], 1)

            def residual(u, g):
                dve.wait_ge(s["o_ps"], g + 1)
                nc.vector.tensor_tensor(acc[:, g, :], at[u][0][:, 0:D], acc[:, g, :], ALU.add).then_inc(s["h2_ok"], 1)
                stats(u, g, acc[:, g, :], 24, "h2_ok", "h2")

            def norm2(u, g, i):
                if later(i):
                    dve.wait_ge(s["xn2_out"], 32 * i)
                normed(u, g, xn2[u][:], acc[:, g, :], 24, "h2", "xn2_ok")

            def logits(u, g):
                dve.wait_ge(s["g_ps"], g + 1)
                nc.vector.tensor_copy(lg[:, g, :], at[u][0][:, 0:E]).then_inc(s["lg_ok"], 1)

            def body(i, proj=True, attn=True):
                b = [2 * i, 2 * i + 1]
                a = [2 * i + 2, 2 * i + 3]
                if proj:
                    embedded(0, a[0])
                if attn:
                    softmax1(0, b[0])
                if proj:
                    normed(0, a[0], xn[0][:], acc[:, a[0], :], 0, "h", "xn_ok")
                    embedded(1, a[1])
                if attn:
                    softmax2(0, b[0])
                    softmax1(1, b[1])
                if proj:
                    normed(1, a[1], xn[1][:], acc[:, a[1], :], 0, "h", "xn_ok")
                    stats(0, a[0], pj[0][0][:, D:D + LAT], 12, "qlat", "l")
                if attn:
                    softmax2(1, b[1])
                if proj:
                    latent(0, a[0])
                if attn:
                    attended(0, b[0])
                if proj:
                    stats(1, a[1], pj[1][0][:, D:D + LAT], 12, "qlat", "l")
                    rope_q(0, a[0])
                    latent(1, a[1])
                if attn:
                    attended(1, b[1])
                    residual(0, b[0])
                if proj:
                    rope_k(0, a[0])
                if attn:
                    norm2(0, b[0], i)
                if proj:
                    rope_q(1, a[1])
                if attn:
                    residual(1, b[1])
                if proj:
                    rope_k(1, a[1])
                if attn:
                    norm2(1, b[1], i)
                if proj:
                    k_blocks(0, a[0])
                if attn:
                    logits(0, b[0])
                if proj:
                    k_blocks(1, a[1])
                if attn:
                    logits(1, b[1])

            dve.wait_ge(s["posb_ok"], 1)
            body(-1, attn=False)
            body(0)
            with dve.Fori(1, PAIRS - 1) as i:
                body(i)
            body(PAIRS - 1, proj=False)

            def shared(g):
                u = g % 2
                dve.wait_ge(s["sh_tanh"], g + 1)
                nc.vector.scalar_tensor_tensor(hs[u][:], th[u][:], 1.0, bank[2 * u][:], ALU.add, ALU.mult).then_inc(s["sh_gate"], 1)
                dve.wait_ge(s["sh_gate"], g + 1)
                nc.vector.scalar_tensor_tensor(hs[u][:], hs[u][:], 0.5, bank[2 * u + 1][:], ALU.mult, ALU.mult).then_inc(s["sh_ok"], 1)

            def shared_add(g):
                dve.wait_ge(s["z_ps"], g + 1)
                nc.vector.tensor_tensor(acc[:, g, :], bank[6 + g % 2][:, 0:D], acc[:, g, :], ALU.add).then_inc(s["acc_ok"], 1)

            steps = [0]

            def step(ins):
                steps[0] += 1
                ins.then_inc(s["route"], 1)
                dve.wait_ge(s["route"], steps[0])

            def e3(ap):
                return ap.rearrange("p (g e) -> p g e", e=E)

            dve.wait_ge(s["lg_ok"], TILES)
            dd, pp, ss, rank, slot = (rt[:, n, :] for n in range(5))
            mx, sm, rs = (sml[:, n, :] for n in range(3))
            step(nc.vector.tensor_reduce(mx, lg[:], AX.X, ALU.max))
            nc.vector.tensor_tensor(e3(dd), lg[:], bc(mx, E, 2), ALU.subtract).then_inc(s["d_max"], 1)
            dve.wait_ge(s["d_exp"], 1)
            step(nc.vector.tensor_reduce(sm, e3(dd), AX.X, ALU.add))
            step(nc.vector.reciprocal(rs, sm))
            step(nc.vector.tensor_tensor(e3(pp), e3(dd), bc(rs, E, 2), ALU.mult))
            step(nc.vector.tensor_tensor(e3(ss), e3(pp), bc(row[:, R_BIAS:R_BIAS + E], TILES, 1), ALU.add))
            r5v = r5.rearrange("p (a f) -> p a f", f=E)
            r6v = r6.rearrange("p (a f) -> p a f", f=E)
            r5q = r5.rearrange("p (g e f) -> p g e f", e=E, f=E)
            r6q = r6.rearrange("p (g e f) -> p g e f", e=E, f=E)
            theirs, own = bc(e3(ss), E, 2), bc(e3(ss), E, 3)
            step(nc.vector.tensor_tensor(r5q, theirs, own, ALU.is_gt))
            step(nc.vector.tensor_tensor(r6q, theirs, own, ALU.is_equal))
            lt = cst[:, C_LT:C_LT + E * E]
            r6m = r6.rearrange("p (g a) -> p g a", a=E * E)
            step(nc.vector.tensor_tensor(r6m, r6m, bc(lt, TILES, 1), ALU.mult))
            step(nc.vector.tensor_tensor(r5, r5, r6, ALU.add))
            step(nc.vector.tensor_reduce(rank, r5v, AX.X, ALU.add))
            sel = rt[:, 5, :]
            for k in range(TOPK):
                step(nc.vector.tensor_scalar(isk[:, k, :], rank, float(k), None, ALU.is_equal))
            step(nc.vector.tensor_tensor(sel, isk[:, 0, :], isk[:, 1, :], ALU.add))
            shared(0)
            dve.wait_ge(s["cnt_ps"], 1)
            cum, tot = bank[7][:, 0:G], rt[:, 6, :]
            step(nc.vector.tensor_copy(tot, bank[7][:, G:2 * G]))
            tot_t = tot.rearrange("p (g e) -> p e g", e=E)
            lt2 = lt.rearrange("p (a b) -> p a b", b=E)
            step(nc.vector.tensor_tensor(r5q, bc(tot_t, TILES, 1), bc(lt2, E, 2), ALU.mult))
            pre = rt[:, 7, :]
            step(nc.vector.tensor_reduce(pre, r5v, AX.X, ALU.add))
            step(nc.vector.tensor_tensor(slot, cum, pre, ALU.add))
            ne, ce, off, end, off128 = (sml[:, n, :] for n in range(3, 8))
            step(nc.vector.tensor_reduce(ne, tot_t, AX.X, ALU.add))
            c64 = r6[:, 0:E * E].rearrange("p (a b) -> p a b", b=E)
            step(nc.vector.tensor_tensor(c64, bc(ne, E, 2), bc(cst[:, C_THR:C_THR + E], E, 1), ALU.is_gt))
            step(nc.vector.tensor_reduce(ce, c64, AX.X, ALU.add))
            step(nc.vector.tensor_tensor(c64, bc(ce, E, 1), lt2, ALU.mult))
            step(nc.vector.tensor_reduce(off, c64, AX.X, ALU.add))
            step(nc.vector.tensor_scalar(off128, off, float(P), None, ALU.mult))
            step(nc.vector.tensor_tensor(e3(slot), e3(slot), bc(off128, TILES, 1), ALU.add))
            shared(1)
            kkv = kk[:].rearrange("p (k a) -> p k a", k=TOPK)
            for n, of in ((0, slot), (1, pp)):
                step(nc.vector.tensor_tensor(kkv, bc(of, TOPK, 1), isk[:], ALU.mult))
                step(nc.vector.tensor_reduce(kv[:, n, :], kk[:].rearrange("p (a e) -> p a e", e=E), AX.X, ALU.add))
            dve.wait_ge(s["ld_init"], 32)
            step(nc.vector.tensor_copy(meta[:].bitcast(F32)[:, :, 2], kv[:, 1, :]))
            step(nc.vector.tensor_copy(ki[:, 0, :], kv[:, 0, :]))
            step(nc.vector.tensor_scalar(ki[:, 1, :], ki[:, 0, :], P - 1, None, ALU.bitwise_and))
            step(nc.vector.tensor_scalar(ki[:, 2, :], ki[:, 0, :], P.bit_length() - 1, None, ALU.logical_shift_right))
            nc.vector.scalar_tensor_tensor(ki[:, 3, :], ki[:, 1, :], float(SLOT_TILES), ki[:, 2, :], ALU.mult,
                                           ALU.add).then_inc(s["routed"], 1)
            step(nc.vector.tensor_tensor(end, off, ce, ALU.add))
            tlv = tl[:].rearrange("p (j e) -> p j e", e=E)
            step(nc.vector.tensor_tensor(tlv, bc(end, SLOT_TILES, 1), bc(cst[:, C_TILE:C_TILE + SLOT_TILES], E, 2), ALU.is_le))
            step(nc.vector.tensor_reduce(tf[:], tlv, AX.X, ALU.add))
            nc.vector.tensor_scalar(ti[:], tf[:], float(E - 1), None, ALU.min).then_inc(s["et_ok"], 1)
            shared_add(0)
            for g in range(2, TILES):
                shared(g)
                shared_add(g - 1)
            shared_add(TILES - 1)
            dve.wait_ge(s["tab_in"], 16)
            gate = kk[:, 0:SLOT_TILES]
            step(nc.vector.tensor_scalar(gate, tb[:].bitcast(F32)[:, :, 2], 0.5, None, ALU.mult))

            def experts(it):
                for u in range(RING):
                    j, b = RING * it + u, u % 2
                    hps = bank[2 + b]
                    dve.wait_ge(s["e_tanh"], j + 1)
                    nc.vector.scalar_tensor_tensor(eh[b], et[b], 1.0, hps[:, 0:INTER], ALU.add, ALU.mult).then_inc(s["e_gate"], 1)
                    dve.wait_ge(s["e_gate"], j + 1)
                    nc.vector.scalar_tensor_tensor(eh[b], eh[b], kk[:, bass.ds(j, 1)], hps[:, INTER:2 * INTER],
                                                   ALU.mult, ALU.mult).then_inc(s["eh_ok"], 1)

            with dve.Fori(0, BLOCKS) as it:
                experts(it)
            for r in range(TILES // 2):
                dve.wait_ge(yg_in[r], 16)
                sum2 = yg[r][:, :, 0, :]
                nc.vector.tensor_tensor(sum2, sum2, yg[r][:, :, 1, :], ALU.add).then_inc(s["f_add"], 1)
                dve.wait_ge(s["f_add"], r + 1)
                a2 = acc[:, 2 * r:2 * r + 2, :]
                nc.vector.tensor_tensor(a2, a2, sum2, ALU.add).then_inc(s["f_ok"], 1)

        @block.tensor
        def _(pe):
            def product(dst, pairs):
                for n, (a, b) in enumerate(pairs):
                    m = nc.tensor.matmul(dst, a, b, start=n == 0, stop=n == len(pairs) - 1)
                return m

            def transposed(dst, src, blocks, done):
                for b in range(blocks):
                    m = nc.tensor.transpose(dst[:, b * P:(b + 1) * P], src[:, b * P:(b + 1) * P], ident)
                m.then_inc(s[done], 1)

            def blocks_of(t, n):
                return [t[:, k * P:(k + 1) * P] for k in range(n)]

            def embed(u, g, i):
                pe.wait_ge(x_in[u], 16 * (i + 2))
                if later(i + 1):
                    pe.wait_ge(s["vx_ok"], 8 * i + 8)
                product(pj[u][0][:, 0:D], [(xt[u][:, k, :], wemb[:, k, :]) for k in range(KF)]).then_inc(s["emb"], 1)

            def xn_t(u, g):
                pe.wait_ge(s["xn_ok"], g + 1)
                transposed(pj[u][1], xn[u], KD, "xnT_ps")

            def q_latent(u, g):
                pe.wait_ge(s["xnT_ok"], g + 1)
                product(pj[u][0][:, 0:D + LAT], list(zip(blocks_of(xnT[u], KD), [wqd[:, k, :] for k in range(KD)])))\
                    .then_inc(s["qlat"], 1)

            def latent_t(u, g):
                pe.wait_ge(s["padded"], 2)
                pe.wait_ge(s["lat_ok"], g + 1)
                nc.tensor.transpose(pj[u][1][0:LAT, 0:P], lat[u][:], ident).then_inc(s["latT_ps"], 1)

            def keys(u, g):
                pe.wait_ge(s["latT_ok"], g + 1)
                product(pj[u][1][:, 0:D], [(latT[u][:], wkv[:, 0:D])]).then_inc(s["k_ps"], 1)

            def values_t(u, g):
                pe.wait_ge(s["qs_ok"], g + 1)
                for hf in range(HALF):
                    m = product(pj[u][0][:, hf * P:(hf + 1) * P], [(wkv[:, D + hf * P:D + (hf + 1) * P], latT[u][:])])
                m.then_inc(s["vT_ps"], 1)

            def q_t(u, g):
                pe.wait_ge(s["qr_ok"], 2 * (g + 1))
                pe.wait_ge(s["ks_ok"], g + 1)
                transposed(pj[u][1], qr[u], HALF, "qT_ps")

            def k_t(u, g):
                pe.wait_ge(s["kr_ok"], 2 * (g + 1))
                pe.wait_ge(s["vT_ok"], g + 1)
                transposed(pj[u][0], kr[u], HALF, "kT_ps")

            def values(u, g):
                for r in range(4):
                    if r == 0:
                        pe.wait_ge(s["qT_ok"], g + 1)
                    elif r == 1:
                        pe.wait_ge(s["kx_ok"], 2 * (g + 1))
                    else:
                        pe.wait_ge(s["vx_ok"], 4 * g + r - 1)
                    for q in range(4):
                        m = nc.tensor.transpose(pj[u][1 - r % 2][:, q * P:(q + 1) * P],
                                                vxT[u][:, 4 * r + q].rearrange("p h k -> p (h k)"), ident)
                    m.then_inc(s["vx_ps"], 1)

            def by_image(b, queries, blocks):
                for hf in range(HALF):
                    for gr in range(GROUPS):
                        c = (hf * GROUPS + gr) * P
                        for n in range(IPG):
                            im = gr * IPG + n
                            m = nc.tensor.matmul(b[n * QG:(n + 1) * QG, c:c + P], queries(hf, im), blocks(hf * IPT + im),
                                                 start=True, stop=True, tile_position=(0, n * QG))
                return m

            def scores(u, g, i):
                pe.wait_ge(s["kx_ok"], 2 * (g + 1))
                pe.wait_ge(s["qT_ok"], g + 1)
                if later(i):
                    pe.wait_ge(s["lg_ok"], 2 * i)
                by_image(at[u][0], lambda hf, im: qT[u][:, hf * P + im * T:hf * P + im * T + QG],
                         lambda n: kx[u][:, n].rearrange("p h k -> p (h k)")).then_inc(s["s_ps"], 1)

            def exps_t(u, g):
                pe.wait_ge(s["s_exp"], g + 1)
                transposed(at[u][1], sc[u], GROUPS * HALF, "pT_ps")

            def attend(u, g):
                pe.wait_ge(s["pT_ok"], g + 1)
                pe.wait_ge(s["vx_ok"], 4 * g + 4)
                by_image(at[u][0], lambda hf, im: pT[u][:, hf * GROUPS * P + im * QG:hf * GROUPS * P + (im + 1) * QG],
                         lambda n: vx[u][:, n, :]).then_inc(s["pv_ps"], 1)

            def attended_t(u, g):
                pe.wait_ge(s["on_ok"], g + 1)
                transposed(at[u][1], on[u], GROUPS * HALF, "oT_ps")

            def o_proj(u, g):
                pe.wait_ge(s["oT_ok"], g + 1)
                product(at[u][0][:, 0:D], list(zip(blocks_of(oT[u], KD), [wo[:, k, :] for k in range(KD)]))).then_inc(s["o_ps"], 1)

            def xn2_t(u, g):
                pe.wait_ge(s["xn2_ok"], g + 1)
                transposed(at[u][1], xn2[u], KD, "xn2T_ps")

            def gate(u, g):
                pe.wait_ge(s["xn2T_ok"], g + 1)
                product(at[u][0][:, 0:P], list(zip(blocks_of(gxT[u], KD), [wgs[:, k, 0:P] for k in range(KD)]))).then_inc(s["g_ps"], 1)

            def body(i, proj=True, attn=True):
                b = [2 * i, 2 * i + 1]
                a = [2 * i + 2, 2 * i + 3]
                if attn:
                    scores(0, b[0], i)
                if proj:
                    embed(0, a[0], i)
                if attn:
                    scores(1, b[1], i)
                if proj:
                    embed(1, a[1], i)
                    xn_t(0, a[0])
                if attn:
                    exps_t(0, b[0])
                if proj:
                    q_latent(0, a[0])
                    xn_t(1, a[1])
                if attn:
                    attend(0, b[0])
                    exps_t(1, b[1])
                if proj:
                    q_latent(1, a[1])
                    latent_t(0, a[0])
                if attn:
                    attend(1, b[1])
                    attended_t(0, b[0])
                if proj:
                    keys(0, a[0])
                    latent_t(1, a[1])
                    values_t(0, a[0])
                if attn:
                    o_proj(0, b[0])
                    attended_t(1, b[1])
                if proj:
                    keys(1, a[1])
                if attn:
                    o_proj(1, b[1])
                    xn2_t(0, b[0])
                if proj:
                    q_t(0, a[0])
                    values_t(1, a[1])
                    k_t(0, a[0])
                if attn:
                    gate(0, b[0])
                if proj:
                    q_t(1, a[1])
                    values(0, a[0])
                if attn:
                    xn2_t(1, b[1])
                if proj:
                    k_t(1, a[1])
                if attn:
                    gate(1, b[1])
                if proj:
                    values(1, a[1])

            pe.wait_ge(s["ld_const"], 32)
            pe.wait_ge(s["ld_emb"], 16)
            pe.wait_ge(s["ld_qd"], 16)
            pe.wait_ge(s["ld_kv"], 16)
            body(-1, attn=False)
            pe.wait_ge(s["ld_o"], 16)
            pe.wait_ge(s["ld_s"], 32)
            body(0)
            with pe.Fori(1, PAIRS - 1) as i:
                body(i)
            body(PAIRS - 1, proj=False)

            def shared_up(g):
                u = g % 2
                if g >= 2:
                    pe.wait_ge(s["sh_ok"], g - 1)
                for n in (0, 1):
                    m = product(bank[2 * u + n][:], [(xn2T[:, g, k * P:(k + 1) * P], wgs[:, k, E + n * SINTER:E + (n + 1) * SINTER])
                                                     for k in range(KD)])
                m.then_inc(s["sh_ps"], 1)

            def shared_t(g):
                pe.wait_ge(s["sh_ok"], g + 1)
                if g >= 2:
                    pe.wait_ge(s["hsT_ok"], g - 1)
                transposed(bank[4 + g % 2], hs[g % 2], KS, "hsT_ps")

            def shared_down(g):
                pe.wait_ge(s["hsT_ok"], g + 1)
                if g >= 2:
                    pe.wait_ge(s["acc_ok"], g - 1)
                if g == 1:
                    pe.wait_ge(s["routed"], 1)
                product(bank[6 + g % 2][:, 0:D], [(hsT[g % 2][:, k * P:(k + 1) * P], ws2[:, k, :]) for k in range(KS)]).then_inc(s["z_ps"], 1)

            pe.wait_ge(s["lg_ok"], TILES)
            pe.wait_ge(s["xn2T_kept"], TILES)
            shared_up(0)
            shared_up(1)
            pe.wait_ge(s["route"], 13)
            product(bank[7][:, 0:G], [(cst[:, C_TRI:C_TRI + P], rt[:, 5, :])])
            product(bank[7][:, G:2 * G], [(cst[:, C_ONE:C_ONE + P], rt[:, 5, :])]).then_inc(s["cnt_ps"], 1)
            shared_t(0)
            for g in range(2, TILES):
                shared_up(g)
                shared_down(g - 2)
                shared_t(g - 1)
            shared_down(TILES - 2)
            shared_t(TILES - 1)
            shared_down(TILES - 1)

            pe.wait_ge(s["ld_e"], 32 * E)
            pe.wait_ge(s["et_ok"], 1)
            pe.wait_ge(s["acc_ok"], TILES)

            def gathered(it, u):
                j = RING * it + u
                pe.wait_ge(gat[u % RING], 16 * (it + 1 + u // RING))
                if u >= 2 or later(it):
                    pe.wait_ge(s["xgT_ok"], j - 1)
                transposed(bank[u % 2], xg[u % RING], KD, "xgT_ps")

            def expert(it, u):
                j = RING * it + u
                col = ti[0:1, j:j + 1] if isinstance(j, int) else ti[0:1, bass.ds(j, 1)]
                return pe.value_load(col, min_val=0, max_val=E - 1)

            def up(it, u):
                j, b = RING * it + u, u % 2
                w = we13[:, expert(it, u), :]
                pe.wait_ge(s["xgT_ok"], j + 1)
                product(bank[2 + b][:], [(xgT[b][:, k * P:(k + 1) * P], w[:, k * 2 * INTER:(k + 1) * 2 * INTER]) for k in range(KD)])\
                    .then_inc(s["eh_ps"], 1)

            def hidden(it, u):
                pe.wait_ge(s["eh_ok"], RING * it + u + 1)
                transposed(bank[4 + u % 2], eh[u % 2], KI, "ehT_ps")

            def down(it, u):
                j, b = RING * it + u, u % 2
                w = we2[:, expert(it, u), :]
                pe.wait_ge(s["ehT_ok"], j + 1)
                product(bank[6 + b][:, 0:D], [(ehT[b][:, k * P:(k + 1) * P], w[:, k * D:(k + 1) * D]) for k in range(KI)])\
                    .then_inc(s["y_ps"], 1)

            def experts(it, first=False, last=False):
                for u in range(RING):
                    if first and u == 0:
                        gathered(0, 0)
                        gathered(0, 1)
                        up(0, 0)
                    if not (last and u == RING - 1):
                        up(it, u + 1)
                    if not (last and u >= RING - 2):
                        gathered(it, u + 2)
                    hidden(it, u)
                    if not (first and u == 0):
                        down(it, u - 1)
                if last:
                    down(it, RING - 1)

            experts(0, first=True)
            with pe.Fori(1, BLOCKS - 1) as it:
                experts(it)
            experts(BLOCKS - 1, last=True)


def constants():
    c = np.zeros((P, C_END), np.float32)
    p = np.arange(P)
    c[:, C_ID:C_ID + P] = np.eye(P)
    c[:, C_TRI:C_TRI + P] = p[:, None] < p[None, :]
    c[:, C_ONE:C_ONE + P] = 1.0
    half = HD // 2
    inv = (1.0 / np.float32(10000.0) ** (np.arange(half, dtype=np.float32) / np.float32(half))).astype(np.float32)
    ang = (p % T).astype(np.float32)[:, None] * inv[None, :]
    cos, sin = np.cos(ang), np.sin(ang)
    both = np.concatenate([cos, cos], 1)
    cross = np.concatenate([sin, -sin], 1)
    scale = 1.0 / np.sqrt(HD)
    c[:, C_CQ:C_CQ + HD], c[:, C_SQ:C_SQ + HD] = both * scale, cross * scale
    c[:, C_CK:C_CK + HD], c[:, C_SK:C_SK + HD] = both, cross
    c[:, C_CAUSAL:C_CAUSAL + T] = np.where(np.arange(T)[None, :] <= (p % T)[:, None], 0.0, -3.0e38)
    e = np.arange(E)
    c[:, C_LT:C_LT + E * E] = (e[None, :] < e[:, None]).reshape(-1)
    c[:, C_THR:C_THR + E] = P * e
    c[:, C_TILE:C_TILE + SLOT_TILES] = np.arange(SLOT_TILES)
    c[:, C_MHALF] = -0.5
    c[:, C_HEAD:C_HEAD + HPH] = p[:, None] // HD == np.arange(HPH)[None, :]
    meta = np.zeros((P, TOPK, TILES, 4), np.int32)
    token = np.arange(TILES)[None, :] * P + p[:, None]
    for k in range(TOPK):
        meta[:, k, :, 0] = token
        meta[:, k, :, 1] = token * TOPK + k
    table = np.zeros((P, SLOT_TILES, 4), np.int32)
    table[:, :, 1] = TOKENS * TOPK + p[:, None] + P * np.arange(SLOT_TILES)[None, :]
    return c, meta.reshape(P, -1), table.reshape(P * SLOT_TILES, 4)


def kernel(x, L0_tok_W, L0_tok_b, L0_tok_pos_emb, L0_attn_W_q, L0_attn_W_dkv, L0_attn_W_uk, L0_attn_W_uv, L0_attn_W_o,
           L0_attn_ln_gamma, L0_attn_ln_beta, L0_ffn_gate_w, L0_ffn_gate_bias, L0_ffn_w1, L0_ffn_w3, L0_ffn_w2,
           L0_ffn_sw1, L0_ffn_sw3, L0_ffn_sw2):
    import concourse.bacc as bacc
    from concourse.bass_utils import run_bass_kernel_spmd

    a = np.asarray

    def blocks(w, k):
        w = a(w)
        return np.ascontiguousarray(w.reshape(k, P, -1).transpose(1, 0, 2).reshape(P, -1))

    def spread(v):
        return np.broadcast_to(a(v)[None, :], (P, a(v).shape[0]))

    xs = a(x).reshape(TILES, IPT, CH, NP, PS, NP, PS).transpose(0, 2, 4, 6, 1, 3, 5).reshape(TILES, KF, P, P)
    c, meta, table = constants()
    ins = {
        "xp": np.ascontiguousarray(xs.transpose(0, 2, 1, 3).reshape(TILES, P, KF * P)),
        "w_emb": blocks(a(L0_tok_W).T, KF),
        "w_qd": blocks(np.concatenate([a(L0_attn_W_q), a(L0_attn_W_dkv)], 1), KD),
        "w_kv": np.ascontiguousarray(np.concatenate([a(L0_attn_W_uk), a(L0_attn_W_uv)], 1)),
        "w_o": blocks(L0_attn_W_o, KD),
        "w_gs": blocks(np.concatenate([a(L0_ffn_gate_w).T, a(L0_ffn_sw1).T, a(L0_ffn_sw3).T], 1), KD),
        "w_s2": blocks(a(L0_ffn_sw2).T, KS),
        "w_e13": np.stack([blocks(np.concatenate([a(L0_ffn_w1)[e].T, a(L0_ffn_w3)[e].T], 1), KD) for e in range(E)]),
        "w_e2": np.stack([blocks(a(L0_ffn_w2)[e].T, KI) for e in range(E)]),
        "rows": np.ascontiguousarray(np.concatenate(
            [np.tile(a(L0_tok_pos_emb), (IPT, 1)), spread(L0_tok_b), spread(L0_attn_ln_gamma), spread(L0_attn_ln_beta),
             spread(L0_ffn_gate_bias)], 1)),
        "consts": c, "meta0": meta, "table0": table,
    }
    nc = bacc.Bacc("TRN2", target_bir_lowering=False, num_devices=1)
    args = [nc.dram_tensor(n, v.shape, mybir.dt.from_np(v.dtype), kind="ExternalInput").ap() for n, v in ins.items()]
    args.append(nc.dram_tensor("out", (TOKENS, D), F32, kind="ExternalOutput").ap())
    build(nc, *args)
    r = run_bass_kernel_spmd(nc, [ins], core_ids=[0])
    return r.results[0]["out"].reshape(IMAGES, T, D)
```

```python
from contextlib import ExitStack

import numpy as np

import concourse.bass as bass
from concourse import mybir

F32 = mybir.dt.float32
F32R = mybir.dt.float32r
I32 = mybir.dt.int32
ALU = mybir.AluOpType
ACT = mybir.ActivationFunctionType
AX = mybir.AxisListType

P = 128
IMAGES, CH, IMG, PS = 64, 3, 64, 16
NP = IMG // PS
T = NP * NP
D = 256
KD = D // P
FEAT = CH * PS * PS
KF = FEAT // P
HEADS, HD = 16, 16
HALF = 2
HPH = HEADS // HALF
LAT = 64
TOKENS = IMAGES * T
TILES = TOKENS // P
IPT = P // T
QG = 32
IPG = P // QG
GROUPS = IPT // IPG
E, INTER, TOPK = 8, 256, 2
KI = INTER // P
SINTER = 2 * INTER
KS = SINTER // P
SLOT_TILES = TOKENS * TOPK // P + E
EPS = 1e-5
RING = 4
BLOCKS = SLOT_TILES // RING

C_ID = 0
C_TRI = C_ID + P
C_ONE = C_TRI + P
C_CQ = C_ONE + P
C_SQ = C_CQ + HD
C_CK = C_SQ + HD
C_SK = C_CK + HD
C_CAUSAL = C_SK + HD
C_LT = C_CAUSAL + T
C_THR = C_LT + E * E
C_TILE = C_THR + E
C_MHALF = C_TILE + SLOT_TILES
C_HEAD = C_MHALF + 1
C_IOTA = C_HEAD + HPH
C_ROW = C_IOTA + P
C_PAD = C_ROW + TOPK * TILES
C_END = C_PAD + SLOT_TILES
R_POS = 0
R_B = R_POS + D
R_GAM = R_B + D
R_BET = R_GAM + LAT
R_BIAS = R_BET + LAT
R_END = R_BIAS + E


def bc(ap, n, at):
    pairs = [list(x) for x in ap.ap]
    shape = list(ap.shape)
    out = ap.unsqueeze(at)
    shape.insert(at, n)
    return out.broadcast_to(shape)


def tile(i, c):
    return 2 * i + c, c % 2, i + c // 2


def exists(g):
    return not isinstance(g, int) or 0 <= g < TILES


def later(n):
    return not isinstance(n, int) or n > 0


def stages(i, c):
    ahead = {"project": 3, "spread": 2, "attend": 1, "close": 0, "gate": -1}
    return {name: tile(i, c + n) for name, n in ahead.items() if exists(tile(i, c + n)[0])}


def slots(engine, slot):
    for c in range(-3, 1):
        slot(0, c)
    with engine.Fori(0, TILES // 2 - 2) as i:
        slot(i, 1)
        slot(i, 2)
    for c in range(TILES - 3, TILES + 1):
        slot(0, c)


def build(nc, xp, w_emb, w_qd, w_kv, w_o, w_gs, w_s2, w_e13, w_e2, rows, consts, out):
    ctx = ExitStack()
    with ctx:
        def sb(name, shape, dt=F32):
            return ctx.enter_context(nc.sbuf_tensor(name, shape, dt))

        def sem(name):
            return ctx.enter_context(nc.semaphore(name))

        bank = [ctx.enter_context(nc.psum_tensor(f"bank{i}", [P, 512], F32)) for i in range(8)]
        pj = [bank[0:2], bank[2:4]]
        at = [bank[4:6], bank[6:8]]

        xn_rows = nc.dram_tensor("xn_rows", (TOKENS, D), F32).ap()
        y_rows = nc.dram_tensor("y_rows", (TOKENS * TOPK + P * SLOT_TILES, D), F32).ap()

        wemb = sb("wemb", [P, KF, D])
        wqd = sb("wqd", [P, KD, D + LAT])
        wkv = sb("wkv", [LAT, 2 * D])
        wo = sb("wo", [P, KD, D])
        wgs = sb("wgs", [P, KD, E + 2 * SINTER])
        ws2 = sb("ws2", [P, KS, D])
        cst = sb("cst", [P, C_END])
        row = sb("row", [P, R_END])
        ident = cst[:, C_ID:C_ID + P]
        xt = [sb(f"xt{u}", [P, KF, P]) for u in (0, 1)]
        posb = sb("posb", [P, D])
        st = [sb(f"st{u}", [P, 40]) for u in (0, 1)]
        xn = [sb(f"xn{u}", [P, D]) for u in (0, 1)]
        xnT = [sb(f"xnT{u}", [P, KD * P]) for u in (0, 1)]
        qc = [sb(f"qc{u}", [P, D]) for u in (0, 1)]
        qs = [sb(f"qs{u}", [P, D]) for u in (0, 1)]
        qr = [sb(f"qr{u}", [P, D]) for u in (0, 1)]
        kc = [sb(f"kc{u}", [P, D]) for u in (0, 1)]
        ks = [sb(f"ks{u}", [P, D]) for u in (0, 1)]
        kr = [sb(f"kr{u}", [P, D]) for u in (0, 1)]
        lat = [sb(f"lat{u}", [P, P]) for u in (0, 1)]
        latg = [sb(f"latg{u}", [P, LAT]) for u in (0, 1)]
        latT = [sb(f"latT{u}", [LAT, P]) for u in (0, 1)]
        qT = [sb(f"qT{u}", [P, HALF * P + QG - T]) for u in (0, 1)]
        pT = [sb(f"pT{u}", [P, GROUPS * HALF * P]) for u in (0, 1)]
        NB = HALF * IPT
        sc = [sb(f"sc{u}", [P, GROUPS * D]) for u in (0, 1)]
        on = [sb(f"on{u}", [P, GROUPS * D]) for u in (0, 1)]
        sx = [sb(f"sx{u}", [P, 3, GROUPS * HEADS]) for u in (0, 1)]
        oT = [sb(f"oT{u}", [P, KD * P]) for u in (0, 1)]
        xn2 = [sb(f"xn2{u}", [P, D]) for u in (0, 1)]
        gxT = [sb(f"gxT{u}", [P, KD * P]) for u in (0, 1)]
        xn2T = sb("xn2T", [P, TILES, KD * P])
        acc = sb("acc", [P, TILES, D])
        hs = [sb(f"hs{u}", [P, SINTER]) for u in (0, 1)]
        lg = sb("lg", [P, TILES, E])
        G = TILES * E
        rt = sb("rt", [P, 8, G])
        r5, r6 = sc[0][:], sc[1][:]
        isk = sb("isk", [P, TOPK, G])
        sml = sb("sml", [P, 8, E])
        kk = sb("kk", [P, TOPK * G])
        kv = sb("kv", [P, 2, TOPK * TILES])
        ki = sb("ki", [P, 3, TOPK * TILES], I32)
        kf = sb("kf", [P, 2, TOPK * TILES])
        tl = sb("tl", [P, SLOT_TILES * E])
        tf = sb("tf", [P, SLOT_TILES])
        ti = sb("ti", [P, SLOT_TILES], I32)
        tb = sb("tb", [P, 3, SLOT_TILES], I32)
        tg = sb("tg", [P, 2, SLOT_TILES])

        with ExitStack() as first:
            def sb_first(name, shape):
                return first.enter_context(nc.sbuf_tensor(name, shape, F32))

            blk = sb_first("blk", [P, 3, 2, NB * P])
            we13 = sb_first("we13", [P, E, KD * 2 * INTER])
            we2 = sb_first("we2", [P, E, KI * D])
            th, hsT = ([sb_first(f"{n}{u}", [P, SINTER]) for u in (0, 1)] for n in ("th", "hsT"))
        we13h, we2h, we13l, we2l = (sb(n, [P, E, w], F32R) for n, w in (
            ("we13h", KD * 2 * INTER), ("we2h", KI * D), ("we13l", KD * 2 * INTER), ("we2l", KI * D)))
        xgT, ehT = ([sb(f"{n}{u}", [P, 2, D], F32R) for u in (0, 1)] for n in ("xgT", "ehT"))
        kx, vxT = ([blk[:, n, u].rearrange("p (a h k) -> p a h k", a=NB, h=HPH) for u in (0, 1)] for n in (0, 1))
        vx = [blk[:, 2, u].rearrange("p (a d) -> p a d", a=NB) for u in (0, 1)]
        blk_flat = blk[:].rearrange("p a b c -> p (a b c)")

        xg = [qc[0][:], qc[1][:], qs[0][:], qs[1][:]]
        ye = [kc[0][:], kc[1][:], ks[0][:], ks[1][:]]
        et, eh = (qr[0][:], qr[1][:]), (kr[0][:], kr[1][:])
        NCH = TOPK * TILES
        lane1 = [t[:].rearrange("p (c l) -> p c l", l=P) for t in (on[0], on[1], pT[0], pT[1])]
        tile1 = xt[0][:].rearrange("p a b -> p (a b)")[:, 0:NCH * SLOT_TILES].rearrange("p (c j) -> p c j", c=NCH)
        what = wemb[:].rearrange("p a b -> p (a b)")[:, 0:(NCH + 1) * 2 * SLOT_TILES]
        what_v = what[:, 0:NCH * 2 * SLOT_TILES].rearrange("p (c n j) -> p c n j", c=NCH, n=2)
        yg = [blk_flat[:, r * 2 * TOPK * D:(r + 1) * 2 * TOPK * D].rearrange("p (g k d) -> p g k d", g=2, k=TOPK)
              for r in range(TILES // 2)]

        names = """ld_const ld_row ld_emb0 ld_emb1 ld_qd ld_kv ld_o ld_s ld_e x_in0 x_in1 padded posb_ok
            emb h_ok h_stat h_aggr h_var h_rstd xn_ok xnT_ps xnT_ok qlat
            qc_ok qs_ok qr_ok l_stat l_aggr l_var l_rstd l_norm l_gam lat_ok latT_ps latT_ok qT_ps qT_ok
            k_ps kc_ok ks_ok kr_ok vT_ps vT_ok kT_ps kx_ok vx_ps vx_ok
            s_ps s_mask s_max s_sub s_exp s_sum s_rec pT_ps pT_ok pv_ps on_ok oT_ps oT_ok o_ps h2_ok
            h2_stat h2_aggr h2_var h2_rstd xn2_ok xn2T_ps xn2T_ok xn2T_kept xn2_free0 xn2_free1 g_ps lg_ok
            sh_ps sh_tanh sh_gate sh_ok hsT_ps hsT_ok z_ps acc_ok
            route d_max d_exp cnt_ps lanes tab_ps tok_ok row_ok et_ok w_high w_low w_low2
            gat0 gat1 gat2 gat3 xgT_ps xgT_hi xgT_ok eh_ps e_tanh e_gate eh_ok ehT_ps ehT_hi ehT_ok y_ps y_ok
            sct0 sct1 sct2 sct3 yg0 yg1 yg2 yg3 f_add f_ok out_a out_b""".split()
        s = {n: sem(n) for n in names}
        x_in = (s["x_in0"], s["x_in1"])
        xn2_free = (s["xn2_free0"], s["xn2_free1"])
        gat = [s[f"gat{r}"] for r in range(RING)]
        sct = [s[f"sct{r}"] for r in range(RING)]
        yg_in = [s[f"yg{r}"] for r in range(4)]
        PAIRS = TILES // 2

        block = ctx.enter_context(nc.Block())

        def heads(ap):
            return ap.rearrange("p (h j d) -> p h j d", h=HEADS, j=2)

        def shared_banks(g):
            return pj[g][0:2] if g < 2 else (at[g % 2][0], at[0][1])

        def vx_bank(u, r):
            return (at[u][1], at[u][0], at[u][1], at[u][1])[r]

        def weight_blocks():
            return ([tuple(w[:, e, :] for w in (we13, we13h, we13l)) for e in range(E)]
                    + [tuple(w[:, e:e + 2, :].rearrange("p e n -> p (e n)") for w in (we2, we2h, we2l))
                       for e in range(0, E, 2)])

        def by_head(ap):
            return ap.rearrange("p (h e) -> p h e", e=HD)

        @block.sync
        def _(sp):
            sp.dma_start(xt[0][:], xp[0]).then_inc(x_in[0], 16)
            sp.dma_start(wemb[:, KF // 2:], w_emb[:, KF // 2 * D:]).then_inc(s["ld_emb1"], 16)
            sp.dma_start(row[:], rows).then_inc(s["ld_row"], 16)
            sp.dma_start(wqd[:], w_qd).then_inc(s["ld_qd"], 16)
            sp.dma_start(wkv[:], w_kv).then_inc(s["ld_kv"], 16)

            def patches(g):
                sp.wait_ge(s["emb"], g - 1)
                sp.dma_start(xt[g % 2][:], xp[g]).then_inc(x_in[g % 2], 16)

            patches(2)
            patches(3)
            sp.dma_start(wo[:], w_o).then_inc(s["ld_o"], 16)
            sp.dma_start(wgs[:], w_gs).then_inc(s["ld_s"], 16)
            sp.dma_start(ws2[:], w_s2).then_inc(s["ld_s"], 16)
            for g in range(TILES):
                if g + 4 < TILES:
                    patches(g + 4)
                sp.dma_start(we13[:, g, :], w_e13[g]).then_inc(s["ld_e"], 16)
                sp.dma_start(we2[:, g, :], w_e2[g]).then_inc(s["ld_e"], 16)
                sp.wait_ge(s["xn2_ok"], g + 1)
                sp.dma_start(xn_rows[g * P:(g + 1) * P, :], xn2[g % 2][:]).then_inc(xn2_free[g % 2], 16)
            for r in range(RING):
                sp.wait_ge(sct[r], 16 * BLOCKS)
            y_tok = y_rows[0:TOKENS * TOPK, :].rearrange("(g p k) d -> p g k d", p=P, k=TOPK)
            for r in range(4):
                sp.dma_start(yg[r], y_tok[:, 2 * r:2 * r + 2]).then_inc(yg_in[r], 16)
            for g in range(0, TILES, 2):
                sp.wait_ge(s["f_ok"], g // 2 + 1)
                sp.dma_start(out[g * P:(g + 1) * P, :], acc[:, g, :]).then_inc(s["out_a"], 16)
            sp.wait_ge(s["out_a"], 16 * PAIRS)
            sp.wait_ge(s["out_b"], 16 * PAIRS)

        @block.gpsimd
        def _(pool):
            for u in (0, 1):
                nc.gpsimd.memset(qT[u][:, HALF * P:], 0.0).then_inc(s["padded"], 1)
                nc.gpsimd.memset(lat[u][:, LAT:], 0.0).then_inc(s["padded"], 1)

            for u in (0, 1):
                nc.gpsimd.memset(xn2[u][:, 0:1], 0.0).then_inc(xn2_free[u], 16)

            def rstd(u, g, src, tag):
                pool.wait_ge(s[tag + "_var"], g + 1)
                nc.gpsimd.tensor_tensor(st[u][:, src + 1:src + 2], st[u][:, src:src + 1], cst[:, C_MHALF:C_MHALF + 1],
                                        ALU.pow).then_inc(s[tag + "_rstd"], 1)

            def latent_affine(u, g):
                pool.wait_ge(s["l_norm"], g + 1)
                nc.gpsimd.tensor_tensor(latg[u][:], lat[u][:, 0:LAT], row[:, R_GAM:R_GAM + LAT], ALU.mult).then_inc(s["l_gam"], 1)
                pool.wait_ge(s["l_gam"], g + 1)
                nc.gpsimd.tensor_tensor(lat[u][:, 0:LAT], latg[u][:], row[:, R_BET:R_BET + LAT], ALU.add).then_inc(s["lat_ok"], 1)

            def slot(i, c):
                now = stages(i, c)
                if "spread" in now:
                    k, uk, _ = now["spread"]
                    pool.wait_ge(s["qs_ok"], k + 1)
                    for j in (0, 1):
                        nc.gpsimd.tensor_tensor(heads(qr[uk][:])[:, :, j, :], heads(qc[uk][:])[:, :, j, :],
                                                heads(qs[uk][:])[:, :, 1 - j, :], ALU.add).then_inc(s["qr_ok"], 1)
                if "project" in now:
                    a, ua, _ = now["project"]
                    rstd(ua, a, 8, "h")
                if "close" in now:
                    o, uo, _ = now["close"]
                    rstd(uo, o, 32, "h2")
                if "project" in now:
                    rstd(ua, a, 20, "l")
                    latent_affine(ua, a)

            pool.wait_ge(s["ld_const"], 16)
            pool.wait_ge(s["ld_row"], 16)
            slots(pool, slot)
            for n, (w, high, low) in enumerate(weight_blocks()[:E]):
                pool.wait_ge(s["w_high"], n + 1)
                nc.gpsimd.tensor_tensor(low, w, high.bitcast(F32), ALU.subtract).then_inc(s["w_low"], 1)
            pool.wait_ge(s["tok_ok"], 1)
            for u in (0, 1):
                pool.wait_ge(xn2_free[u], 16 * (1 + TILES // 2))

            def gather(j):
                nc.gpsimd.indirect_dma_start(
                    out=xg[j % RING], out_offset=None, in_=xn_rows,
                    in_offset=bass.IndirectOffsetOnAxis(ap=tb[:, 1, j:j + 1], axis=0)).then_inc(gat[j % RING], 16)

            def scatter(j):
                pool.wait_ge(s["y_ok"], j + 1)
                nc.gpsimd.indirect_dma_start(
                    out=y_rows, out_offset=bass.IndirectOffsetOnAxis(ap=tb[:, 2, j:j + 1], axis=0),
                    in_=ye[j % RING], in_offset=None).then_inc(sct[j % RING], 16)

            for j in range(RING):
                gather(j)
            pool.wait_ge(s["row_ok"], 1)
            for j in range(SLOT_TILES):
                if j + RING < SLOT_TILES:
                    pool.wait_ge(s["xgT_ps"], j + 1)
                    gather(j + RING)
                if j >= RING - 1:
                    scatter(j - RING + 1)
            for j in range(SLOT_TILES - RING + 1, SLOT_TILES):
                scatter(j)

        @block.scalar
        def _(act):
            act.dma_start(wemb[:, 0:KF // 2], w_emb[:, 0:KF // 2 * D]).then_inc(s["ld_emb0"], 16)
            act.dma_start(cst[:], consts).then_inc(s["ld_const"], 16)
            act.dma_start(xt[1][:], xp[1]).then_inc(x_in[1], 16)

            def copy(dst, src, ready, at, done):
                act.wait_ge(s[ready], at)
                nc.scalar.copy(dst, src).then_inc(s[done], 1)

            def v_blocks(u, g, hds):
                if hds[0] == 0:
                    act.wait_ge(s["padded"], 4)
                    act.wait_ge(s["vT_ps"], g + 1)
                for hd in hds:
                    m = nc.scalar.activation(vxT[u][:, :, hd, :], pj[u][0][:, 0:D].rearrange("p (a k) -> p a k", k=T),
                                             ACT.Copy, scale=cst[:, C_HEAD + hd:C_HEAD + hd + 1])
                if hds[-1] == HPH - 1:
                    m.then_inc(s["vT_ok"], 1)

            def vx_round(u, g, r):
                copy(vx[u][:, 4 * r:4 * r + 4, :].rearrange("p a b -> p (a b)"), vx_bank(u, r)[:],
                     "vx_ps", 4 * g + r + 1, "vx_ok")

            def exp(u, g):
                act.wait_ge(s["s_sub"], g + 1)
                nc.scalar.activation(sc[u][:], sc[u][:], ACT.Exp).then_inc(s["s_exp"], 1)

            def pT_copy(u, g):
                copy(pT[u][:], at[u][1][:], "pT_ps", g + 1, "pT_ok")

            def oT_copy(u, g):
                copy(oT[u][:].rearrange("p (i q) -> p i q", q=T), at[u][1][:].rearrange("p (i q) -> p i q", q=QG)[:, :, 0:T],
                     "oT_ps", g + 1, "oT_ok")

            def slot(i, c):
                now = stages(i, c)
                if "attend" in now:
                    q, uq, _ = now["attend"]
                    vx_round(uq, q, 0)
                if "spread" in now:
                    k, uk, _ = now["spread"]
                    copy(latT[uk][:], pj[uk][1][0:LAT, 0:P], "latT_ps", k + 1, "latT_ok")
                if "attend" in now:
                    vx_round(uq, q, 1)
                    vx_round(uq, q, 2)
                if "spread" in now:
                    v_blocks(uk, k, (0, 1, 2, 3))
                if "attend" in now:
                    vx_round(uq, q, 3)
                if "close" in now:
                    o, uo, _ = now["close"]
                    oT_copy(uo, o)
                if c == TILES - 1:
                    shared_T(1)
                if "spread" in now:
                    v_blocks(uk, k, (4, 5))
                if "project" in now:
                    a, ua, _ = now["project"]
                    copy(xnT[ua][:], pj[ua][1][:, 0:D], "xnT_ps", a + 1, "xnT_ok")
                if c == TILES - 2:
                    shared_T(0)
                if "attend" in now:
                    exp(uq, q)
                if "spread" in now:
                    v_blocks(uk, k, (6, 7))
                if "attend" in now:
                    pT_copy(uq, q)
                if c in (TILES - 3, TILES - 2):
                    shared(c - (TILES - 3))
                if "spread" in now:
                    copy(qT[uk][:, 0:D], pj[uk][0][:, 0:D], "qT_ps", k + 1, "qT_ok")
                if "close" in now:
                    copy(gxT[uo][:], at[uo][1][:, 0:D], "xn2T_ps", o + 1, "xn2T_ok")
                    nc.scalar.copy(xn2T[:, o, :], at[uo][1][:, 0:D]).then_inc(s["xn2T_kept"], 1)

            def shared(g):
                act.wait_ge(s["sh_ps"], g + 1)
                nc.scalar.activation(th[g % 2][:], pj[g % 2][0][:], ACT.Tanh, scale=0.5).then_inc(s["sh_tanh"], 1)

            def shared_T(g):
                copy(hsT[g % 2][:], shared_banks(g)[0][:], "hsT_ps", g + 1, "hsT_ok")

            slots(act, slot)

            act.wait_ge(s["d_max"], 1)
            nc.scalar.activation(rt[:, 0, :], rt[:, 0, :], ACT.Exp).then_inc(s["d_exp"], 1)
            act.wait_ge(s["ld_e"], 32 * E)
            blocks = iter(weight_blocks())

            def high_part():
                w, high, _ = next(blocks)
                nc.scalar.copy(high, w).then_inc(s["w_high"], 1)

            for _ in range(4):
                high_part()
            shared(2)
            high_part()
            for g in range(3, TILES):
                shared(g)
                shared_T(g - 1)
                for _ in range(3 if g < 5 else 1 if g < 6 else 0):
                    high_part()
            shared_T(TILES - 1)

            def experts(it, first=False, last=False):
                for u in range(RING):
                    j, b = RING * it + u, u % 2
                    if first and u == 0:
                        copy(xgT[0][:, 0, :], bank[0][:, 0:D], "xgT_ps", 1, "xgT_hi")
                        copy(xgT[1][:, 0, :], bank[1][:, 0:D], "xgT_ps", 2, "xgT_hi")
                        tanh(0, 0)
                        copy(xgT[0][:, 0, :], bank[0][:, 0:D], "xgT_ps", 3, "xgT_hi")
                    if not (last and u == RING - 1):
                        tanh(j + 1, 1 - b)
                    if not (last and u >= RING - 3):
                        copy(xgT[1 - b][:, 0, :], bank[1 - b][:, 0:D], "xgT_ps", j + 4, "xgT_hi")
                    copy(ehT[b][:, 0, :], bank[4 + b][:, 0:INTER], "ehT_ps", j + 1, "ehT_hi")
                    if not (first and u == 0):
                        result(it, u - 1)
                if last:
                    result(it, RING - 1)

            def tanh(j, b):
                act.wait_ge(s["eh_ps"], j + 1)
                nc.scalar.activation(et[b], bank[2 + b][:, 0:INTER], ACT.Tanh, scale=0.5).then_inc(s["e_tanh"], 1)

            def result(it, u):
                j, b = RING * it + u, u % 2
                n = it if u >= 0 else it - 1
                if later(n):
                    act.wait_ge(sct[u % RING], 16 * n)
                copy(ye[u % RING], bank[6 + b][:, 0:D], "y_ps", j + 1, "y_ok")

            experts(0, first=True)
            experts(1)
            with act.Fori(2, BLOCKS - 1) as it:
                experts(it)
            experts(BLOCKS - 1, last=True)
            for g in range(1, TILES, 2):
                act.wait_ge(s["f_ok"], g // 2 + 1)
                act.dma_start(out[g * P:(g + 1) * P, :], acc[:, g, :]).then_inc(s["out_b"], 16)

        @block.vector
        def _(dve):
            dve.wait_ge(s["ld_const"], 16)
            dve.wait_ge(s["ld_row"], 16)
            nc.vector.tensor_tensor(posb[:], row[:, R_POS:R_POS + D], row[:, R_B:R_B + D], ALU.add).then_inc(s["posb_ok"], 1)

            def stats(u, g, src, col, ready, tag):
                dve.wait_ge(s["posb_ok"], 1)
                dve.wait_ge(s[ready], g + 1)
                nc.vector.bn_stats(st[u][:, col:col + 6], src).then_inc(s[tag + "_stat"], 1)
                dve.wait_ge(s["posb_ok"], 1)
                dve.wait_ge(s[tag + "_stat"], g + 1)
                nc.vector.bn_aggr(st[u][:, col + 6:col + 8], st[u][:, col:col + 6]).then_inc(s[tag + "_aggr"], 1)
                dve.wait_ge(s[tag + "_aggr"], g + 1)
                nc.vector.tensor_scalar(st[u][:, col + 8:col + 9], st[u][:, col + 7:col + 8], EPS, None,
                                        ALU.add).then_inc(s[tag + "_var"], 1)

            def normed(u, g, dst, src, col, tag, done):
                dve.wait_ge(s[tag + "_rstd"], g + 1)
                nc.vector.tensor_scalar(dst, src, st[u][:, col + 6:col + 7], st[u][:, col + 9:col + 10],
                                        ALU.subtract, ALU.mult).then_inc(s[done], 1)

            def embedded(u, g):
                dve.wait_ge(s["emb"], g + 1)
                nc.vector.tensor_tensor(acc[:, g, :], pj[u][0][:, 0:D], posb[:], ALU.add).then_inc(s["h_ok"], 1)
                stats(u, g, acc[:, g, :], 0, "h_ok", "h")

            def latent(u, g):
                normed(u, g, lat[u][:, 0:LAT], pj[u][0][:, D:D + LAT], 12, "l", "l_norm")

            def turn(u, ps, dst, col, ok):
                nc.vector.tensor_tensor(by_head(dst[u][:]), by_head(ps), bc(cst[:, col:col + HD], HEADS, 1),
                                        ALU.mult).then_inc(s[ok], 1)

            def turned(u, g, c, sn, r, tag):
                dve.wait_ge(s[tag + "s_ok"], g + 1)
                for j in (0, 1):
                    nc.vector.tensor_tensor(heads(r[u][:])[:, :, j, :], heads(c[u][:])[:, :, j, :],
                                            heads(sn[u][:])[:, :, 1 - j, :], ALU.add).then_inc(s[tag + "r_ok"], 1)

            def rope_q(u, g):
                turn(u, pj[u][0][:, 0:D], qc, C_CQ, "qc_ok")
                turn(u, pj[u][0][:, 0:D], qs, C_SQ, "qs_ok")

            def k_blocks(u, g, hf):
                dve.wait_ge(s["kT_ps"], g + 1)
                kT = pj[u][1][:, hf * P:(hf + 1) * P].rearrange("p (i k) -> p i k", k=T)
                of = bc(bc(cst[:, C_HEAD:C_HEAD + HPH], T, 2), IPT, 1)
                nc.vector.tensor_tensor(kx[u][:, hf * IPT:(hf + 1) * IPT], bc(kT, HPH, 2), of, ALU.mult).then_inc(s["kx_ok"], 1)

            def masked(u, g):
                dve.wait_ge(s["s_ps"], g + 1)
                nc.vector.tensor_tensor(by_head(sc[u][:]), by_head(at[u][0][:]),
                                        bc(cst[:, C_CAUSAL:C_CAUSAL + T], GROUPS * HEADS, 1), ALU.add).then_inc(s["s_mask"], 1)

            def row_max(u, g):
                dve.wait_ge(s["s_mask"], g + 1)
                nc.vector.tensor_reduce(sx[u][:, 0, :], by_head(sc[u][:]), AX.X, ALU.max).then_inc(s["s_max"], 1)

            def less_max(u, g):
                dve.wait_ge(s["s_max"], g + 1)
                nc.vector.tensor_tensor(by_head(sc[u][:]), by_head(sc[u][:]), bc(sx[u][:, 0, :], T, 2),
                                        ALU.subtract).then_inc(s["s_sub"], 1)

            def row_sum(u, g):
                dve.wait_ge(s["s_exp"], g + 1)
                nc.vector.tensor_reduce(sx[u][:, 1, :], by_head(sc[u][:]), AX.X, ALU.add).then_inc(s["s_sum"], 1)

            def row_factor(u, g):
                dve.wait_ge(s["s_sum"], g + 1)
                nc.vector.reciprocal(sx[u][:, 2, :], sx[u][:, 1, :]).then_inc(s["s_rec"], 1)

            def attended(u, g):
                dve.wait_ge(s["s_rec"], g + 1)
                dve.wait_ge(s["pv_ps"], g + 1)
                nc.vector.tensor_tensor(by_head(on[u][:]), by_head(at[u][0][:]), bc(sx[u][:, 2, :], HD, 2), ALU.mult)\
                    .then_inc(s["on_ok"], 1)

            def residual(u, g):
                dve.wait_ge(s["o_ps"], g + 1)
                nc.vector.tensor_tensor(acc[:, g, :], at[u][0][:, 0:D], acc[:, g, :], ALU.add).then_inc(s["h2_ok"], 1)

            def norm2(u, g, n):
                dve.wait_ge(xn2_free[u], 16 * (n + 1))
                normed(u, g, xn2[u][:], acc[:, g, :], 24, "h2", "xn2_ok")

            def logits(u, g):
                dve.wait_ge(s["g_ps"], g + 1)
                nc.vector.tensor_copy(lg[:, g, :], at[u][0][:, 0:E]).then_inc(s["lg_ok"], 1)

            def slot(i, c):
                now = stages(i, c)
                if "close" in now:
                    o, uo, no = now["close"]
                    attended(uo, o)
                if "spread" in now:
                    k, uk, _ = now["spread"]
                    turn(uk, pj[uk][0][:, 0:D], qc, C_CQ, "qc_ok")
                if "gate" in now:
                    p, up, _ = now["gate"]
                    logits(up, p)
                if "spread" in now:
                    turn(uk, pj[uk][0][:, 0:D], qs, C_SQ, "qs_ok")
                if "project" in now:
                    a, ua, _ = now["project"]
                    embedded(ua, a)
                if "attend" in now:
                    q, uq, _ = now["attend"]
                    masked(uq, q)
                if "project" in now:
                    normed(ua, a, xn[ua][:], acc[:, a, :], 0, "h", "xn_ok")
                if "attend" in now:
                    row_max(uq, q)
                if "spread" in now:
                    dve.wait_ge(s["k_ps"], k + 1)
                    turn(uk, pj[uk][1][:, 0:D], kc, C_CK, "kc_ok")
                if "attend" in now:
                    less_max(uq, q)
                if "spread" in now:
                    turn(uk, pj[uk][1][:, 0:D], ks, C_SK, "ks_ok")
                if "close" in now:
                    residual(uo, o)
                if "spread" in now:
                    turned(uk, k, kc, ks, kr, "k")
                if "close" in now:
                    stats(uo, o, acc[:, o, :], 24, "h2_ok", "h2")
                if "project" in now:
                    stats(ua, a, pj[ua][0][:, D:D + LAT], 12, "qlat", "l")
                if "attend" in now:
                    row_sum(uq, q)
                if "close" in now:
                    norm2(uo, o, no)
                if "spread" in now:
                    k_blocks(uk, k, 0)
                if "attend" in now:
                    row_factor(uq, q)
                if "project" in now:
                    latent(ua, a)
                if "spread" in now:
                    k_blocks(uk, k, 1)
                if c == TILES - 3:
                    shared(0)
                if c == TILES - 2:
                    shared(1)
                    shared_add(0)
                if c == TILES:
                    shared_add(1)

            def shared(g):
                u = g % 2
                dve.wait_ge(s["sh_tanh"], g + 1)
                nc.vector.scalar_tensor_tensor(hs[u][:], th[u][:], 1.0, pj[u][0][:], ALU.add, ALU.mult).then_inc(s["sh_gate"], 1)
                dve.wait_ge(s["sh_gate"], g + 1)
                nc.vector.scalar_tensor_tensor(hs[u][:], hs[u][:], 0.5, pj[u][1][:], ALU.mult, ALU.mult).then_inc(s["sh_ok"], 1)

            def shared_add(g):
                dve.wait_ge(s["z_ps"], g + 1)
                nc.vector.tensor_tensor(acc[:, g, :], shared_banks(g)[1][:, 0:D], acc[:, g, :], ALU.add).then_inc(s["acc_ok"], 1)

            dve.wait_ge(s["posb_ok"], 1)
            slots(dve, slot)

            steps = [0]

            def step(ins):
                steps[0] += 1
                ins.then_inc(s["route"], 1)
                dve.wait_ge(s["route"], steps[0])

            def e3(ap):
                return ap.rearrange("p (g e) -> p g e", e=E)

            dve.wait_ge(s["lg_ok"], TILES)
            dd, pp, ss, rank, slot = (rt[:, n, :] for n in range(5))
            mx, sm, rs = (sml[:, n, :] for n in range(3))
            step(nc.vector.tensor_reduce(mx, lg[:], AX.X, ALU.max))
            nc.vector.tensor_tensor(e3(dd), lg[:], bc(mx, E, 2), ALU.subtract).then_inc(s["d_max"], 1)
            dve.wait_ge(s["d_exp"], 1)
            step(nc.vector.tensor_reduce(sm, e3(dd), AX.X, ALU.add))
            step(nc.vector.reciprocal(rs, sm))
            step(nc.vector.tensor_tensor(e3(pp), e3(dd), bc(rs, E, 2), ALU.mult))
            step(nc.vector.tensor_tensor(e3(ss), e3(pp), bc(row[:, R_BIAS:R_BIAS + E], TILES, 1), ALU.add))
            r5v = r5.rearrange("p (a f) -> p a f", f=E)
            r6v = r6.rearrange("p (a f) -> p a f", f=E)
            r5q = r5.rearrange("p (g e f) -> p g e f", e=E, f=E)
            r6q = r6.rearrange("p (g e f) -> p g e f", e=E, f=E)
            theirs, own = bc(e3(ss), E, 2), bc(e3(ss), E, 3)
            step(nc.vector.tensor_tensor(r5q, theirs, own, ALU.is_gt))
            step(nc.vector.tensor_tensor(r6q, theirs, own, ALU.is_equal))
            lt = cst[:, C_LT:C_LT + E * E]
            r6m = r6.rearrange("p (g a) -> p g a", a=E * E)
            step(nc.vector.tensor_tensor(r6m, r6m, bc(lt, TILES, 1), ALU.mult))
            step(nc.vector.tensor_tensor(r5, r5, r6, ALU.add))
            step(nc.vector.tensor_reduce(rank, r5v, AX.X, ALU.add))
            sel = rt[:, 5, :]
            for k in range(TOPK):
                step(nc.vector.tensor_scalar(isk[:, k, :], rank, float(k), None, ALU.is_equal))
            step(nc.vector.tensor_tensor(sel, isk[:, 0, :], isk[:, 1, :], ALU.add))
            shared(2)
            dve.wait_ge(s["cnt_ps"], 1)
            cum, tot = bank[7][:, 0:G], rt[:, 6, :]
            step(nc.vector.tensor_copy(tot, bank[7][:, G:2 * G]))
            tot_t = tot.rearrange("p (g e) -> p e g", e=E)
            lt2 = lt.rearrange("p (a b) -> p a b", b=E)
            step(nc.vector.tensor_tensor(r5q, bc(tot_t, TILES, 1), bc(lt2, E, 2), ALU.mult))
            pre = rt[:, 7, :]
            step(nc.vector.tensor_reduce(pre, r5v, AX.X, ALU.add))
            step(nc.vector.tensor_tensor(slot, cum, pre, ALU.add))
            ne, ce, off, end, off128 = (sml[:, n, :] for n in range(3, 8))
            step(nc.vector.tensor_reduce(ne, tot_t, AX.X, ALU.add))
            c64 = r6[:, 0:E * E].rearrange("p (a b) -> p a b", b=E)
            step(nc.vector.tensor_tensor(c64, bc(ne, E, 2), bc(cst[:, C_THR:C_THR + E], E, 1), ALU.is_gt))
            step(nc.vector.tensor_reduce(ce, c64, AX.X, ALU.add))
            step(nc.vector.tensor_tensor(c64, bc(ce, E, 1), lt2, ALU.mult))
            step(nc.vector.tensor_reduce(off, c64, AX.X, ALU.add))
            step(nc.vector.tensor_scalar(off128, off, float(P), None, ALU.mult))
            step(nc.vector.tensor_tensor(e3(slot), e3(slot), bc(off128, TILES, 1), ALU.add))
            shared(3)
            kkv = kk[:].rearrange("p (k a) -> p k a", k=TOPK)
            for n, of in ((0, slot), (1, pp)):
                step(nc.vector.tensor_tensor(kkv, bc(of, TOPK, 1), isk[:], ALU.mult))
                step(nc.vector.tensor_reduce(kv[:, n, :], kk[:].rearrange("p (a e) -> p a e", e=E), AX.X, ALU.add))
            step(nc.vector.tensor_copy(ki[:, 0, :], kv[:, 0, :]))
            step(nc.vector.tensor_scalar(ki[:, 1, :], ki[:, 0, :], P - 1, None, ALU.bitwise_and))
            step(nc.vector.tensor_scalar(ki[:, 2, :], ki[:, 0, :], P.bit_length() - 1, None, ALU.logical_shift_right))
            step(nc.vector.tensor_copy(kf[:], ki[:, 1:3, :]))
            lane, tileno = kf[:, 0, :], kf[:, 1, :]
            step(nc.vector.tensor_tensor(tile1, bc(tileno, SLOT_TILES, 2), bc(cst[:, C_TILE:C_TILE + SLOT_TILES], NCH, 1), ALU.is_equal))
            nc.vector.tensor_tensor(what_v[:, :, 0, :], tile1, bc(cst[:, C_ROW:C_ROW + NCH], SLOT_TILES, 2), ALU.mult).then_inc(s["lanes"], 1)
            nc.vector.tensor_tensor(what_v[:, :, 1, :], tile1, bc(kv[:, 1, :], SLOT_TILES, 2), ALU.mult).then_inc(s["lanes"], 1)
            nc.vector.memset(what[:, NCH * 2 * SLOT_TILES:], 0.0).then_inc(s["lanes"], 1)
            for n in range(4):
                ch = slice(n * NCH // 4, (n + 1) * NCH // 4)
                nc.vector.tensor_tensor(lane1[n], bc(lane[:, ch], P, 2), bc(cst[:, C_IOTA:C_IOTA + P], NCH // 4, 1),
                                        ALU.is_equal).then_inc(s["lanes"], 1)
            shared_add(2)
            shared(4)
            dve.wait_ge(s["tab_ps"], 1)
            row1, gates = bank[7][:, 256:256 + SLOT_TILES], bank[7][:, 256 + SLOT_TILES:256 + 2 * SLOT_TILES]
            step(nc.vector.tensor_scalar(tb[:, 0, :], row1, -1.0, 0.0, ALU.add, ALU.max))
            nc.vector.tensor_scalar(tb[:, 1, :], tb[:, 0, :], TOPK.bit_length() - 1, None, ALU.logical_shift_right).then_inc(s["tok_ok"], 1)
            step(nc.vector.scalar_tensor_tensor(tg[:, 0, :], row1, 0.0, cst[:, C_PAD:C_PAD + SLOT_TILES], ALU.is_equal, ALU.mult))
            nc.vector.scalar_tensor_tensor(tb[:, 2, :], row1, -1.0, tg[:, 0, :], ALU.add, ALU.add).then_inc(s["row_ok"], 1)
            step(nc.vector.tensor_scalar(tg[:, 1, :], gates, 0.5, None, ALU.mult))
            step(nc.vector.tensor_tensor(end, off, ce, ALU.add))
            tlv = tl[:].rearrange("p (j e) -> p j e", e=E)
            step(nc.vector.tensor_tensor(tlv, bc(end, SLOT_TILES, 1), bc(cst[:, C_TILE:C_TILE + SLOT_TILES], E, 2), ALU.is_le))
            step(nc.vector.tensor_reduce(tf[:], tlv, AX.X, ALU.add))
            nc.vector.tensor_scalar(ti[:], tf[:], float(E - 1), None, ALU.min).then_inc(s["et_ok"], 1)
            lows = iter(list(enumerate(weight_blocks()))[E:])
            for g in range(4, TILES):
                if g > 4:
                    shared(g)
                n, (w, high, low) = next(lows)
                dve.wait_ge(s["w_high"], n + 1)
                nc.vector.tensor_tensor(low, w, high.bitcast(F32), ALU.subtract).then_inc(s["w_low2"], 1)
                shared_add(g - 1)

            def low(dst, src, at, done, got):
                dve.wait_ge(s[got], at)
                nc.vector.tensor_tensor(dst[:, 1, :], src, dst[:, 0, :].bitcast(F32), ALU.subtract).then_inc(s[done], 1)

            def hidden(j, b):
                hps = bank[2 + b]
                dve.wait_ge(s["e_tanh"], j + 1)
                nc.vector.scalar_tensor_tensor(eh[b], et[b], 1.0, hps[:, 0:INTER], ALU.add, ALU.mult).then_inc(s["e_gate"], 1)
                dve.wait_ge(s["e_gate"], j + 1)
                nc.vector.scalar_tensor_tensor(eh[b], eh[b], tg[:, 1, j:j + 1] if isinstance(j, int) else tg[:, 1, bass.ds(j, 1)],
                                               hps[:, INTER:2 * INTER], ALU.mult, ALU.mult).then_inc(s["eh_ok"], 1)

            def experts(it, first=False, last=False):
                for u in range(RING):
                    j, b = RING * it + u, u % 2
                    if first and u == 0:
                        low(xgT[0], bank[0][:, 0:D], 1, "xgT_ok", "xgT_hi")
                        low(xgT[1], bank[1][:, 0:D], 2, "xgT_ok", "xgT_hi")
                        shared_add(TILES - 1)
                        hidden(0, 0)
                        low(xgT[0], bank[0][:, 0:D], 3, "xgT_ok", "xgT_hi")
                    if not (last and u == RING - 1):
                        hidden(j + 1, 1 - b)
                    if not (last and u >= RING - 3):
                        low(xgT[1 - b], bank[1 - b][:, 0:D], j + 4, "xgT_ok", "xgT_hi")
                    low(ehT[b], bank[4 + b][:, 0:INTER], j + 1, "ehT_ok", "ehT_hi")

            experts(0, first=True)
            with dve.Fori(1, BLOCKS - 1) as it:
                experts(it)
            experts(BLOCKS - 1, last=True)
            for r in range(TILES // 2):
                dve.wait_ge(yg_in[r], 16)
                sum2 = yg[r][:, :, 0, :]
                nc.vector.tensor_tensor(sum2, sum2, yg[r][:, :, 1, :], ALU.add).then_inc(s["f_add"], 1)
                dve.wait_ge(s["f_add"], r + 1)
                a2 = acc[:, 2 * r:2 * r + 2, :]
                nc.vector.tensor_tensor(a2, a2, sum2, ALU.add).then_inc(s["f_ok"], 1)

        @block.tensor
        def _(pe):
            def product(dst, pairs):
                for n, (a, b) in enumerate(pairs):
                    m = nc.tensor.matmul(dst, a, b, start=n == 0, stop=n == len(pairs) - 1)
                return m

            def transposed(dst, src, blocks, done):
                for b in range(blocks):
                    m = nc.tensor.transpose(dst[:, b * P:(b + 1) * P], src[:, b * P:(b + 1) * P], ident)
                m.then_inc(s[done], 1)

            def blocks_of(t, n):
                return [t[:, k * P:(k + 1) * P] for k in range(n)]

            def embed(u, g, n, first):
                pe.wait_ge(x_in[u], 16 * (n + 1))
                if later(n):
                    pe.wait_ge(s["qT_ok"], g - 1)
                for k in range(KF):
                    if first and k == KF // 2:
                        pe.wait_ge(s["ld_emb1"], 16)
                    m = nc.tensor.matmul(pj[u][0][:, 0:D], xt[u][:, k, :], wemb[:, k, :], start=k == 0, stop=k == KF - 1)
                m.then_inc(s["emb"], 1)
                if first:
                    pe.wait_ge(s["ld_const"], 16)
                    pe.wait_ge(s["ld_qd"], 16)
                    pe.wait_ge(s["ld_kv"], 16)
                    pe.wait_ge(s["padded"], 4)

            def xn_t(u, g, n):
                pe.wait_ge(s["xn_ok"], g + 1)
                if later(n):
                    pe.wait_ge(s["kx_ok"], 2 * g - 2)
                transposed(pj[u][1], xn[u], KD, "xnT_ps")

            def q_latent(u, g):
                pe.wait_ge(s["xnT_ok"], g + 1)
                product(pj[u][0][:, 0:D + LAT], list(zip(blocks_of(xnT[u], KD), [wqd[:, k, :] for k in range(KD)])))\
                    .then_inc(s["qlat"], 1)

            def latent_t(u, g):
                pe.wait_ge(s["lat_ok"], g + 1)
                nc.tensor.transpose(pj[u][1][:, 0:P], lat[u][:], ident).then_inc(s["latT_ps"], 1)

            def values_t(u, g):
                pe.wait_ge(s["latT_ok"], g + 1)
                pe.wait_ge(s["qs_ok"], g + 1)
                for hf in range(HALF):
                    m = product(pj[u][0][:, hf * P:(hf + 1) * P], [(wkv[:, D + hf * P:D + (hf + 1) * P], latT[u][:])])
                m.then_inc(s["vT_ps"], 1)

            def keys(u, g):
                product(pj[u][1][:, 0:D], [(latT[u][:], wkv[:, 0:D])]).then_inc(s["k_ps"], 1)

            def k_t(u, g):
                pe.wait_ge(s["kr_ok"], 2 * (g + 1))
                transposed(pj[u][1], kr[u], HALF, "kT_ps")

            def q_t(u, g):
                pe.wait_ge(s["qr_ok"], 2 * (g + 1))
                pe.wait_ge(s["vT_ok"], g + 1)
                transposed(pj[u][0], qr[u], HALF, "qT_ps")

            def values(u, g, n, rounds):
                for r in rounds:
                    if r == 0 and later(n):
                        pe.wait_ge(s["xn2T_kept"], g - 1)
                    elif r == 1 and later(n):
                        pe.wait_ge(s["lg_ok"], g - 1)
                    elif r == 2:
                        pe.wait_ge(s["vx_ok"], 4 * g + 1)
                    elif r == 3:
                        pe.wait_ge(s["vx_ok"], 4 * g + 3)
                    for q in range(4):
                        m = nc.tensor.transpose(vx_bank(u, r)[:, q * P:(q + 1) * P],
                                                vxT[u][:, 4 * r + q].rearrange("p h k -> p (h k)"), ident)
                    m.then_inc(s["vx_ps"], 1)

            def by_image(b, queries, blocks):
                for hf in range(HALF):
                    for gr in range(GROUPS):
                        c = (hf * GROUPS + gr) * P
                        for n in range(IPG):
                            im = gr * IPG + n
                            m = nc.tensor.matmul(b[n * QG:(n + 1) * QG, c:c + P], queries(hf, im), blocks(hf * IPT + im),
                                                 start=True, stop=True, tile_position=(0, n * QG))
                return m

            def scores(u, g):
                pe.wait_ge(s["kx_ok"], 2 * (g + 1))
                pe.wait_ge(s["qT_ok"], g + 1)
                pe.wait_ge(s["vx_ok"], 4 * g + 2)
                by_image(at[u][0], lambda hf, im: qT[u][:, hf * P + im * T:hf * P + im * T + QG],
                         lambda n: kx[u][:, n].rearrange("p h k -> p (h k)")).then_inc(s["s_ps"], 1)

            def exps_t(u, g):
                pe.wait_ge(s["s_exp"], g + 1)
                pe.wait_ge(s["vx_ok"], 4 * g + 4)
                transposed(at[u][1], sc[u], GROUPS * HALF, "pT_ps")

            def attend(u, g):
                pe.wait_ge(s["pT_ok"], g + 1)
                by_image(at[u][0], lambda hf, im: pT[u][:, hf * GROUPS * P + im * QG:hf * GROUPS * P + (im + 1) * QG],
                         lambda n: vx[u][:, n, :]).then_inc(s["pv_ps"], 1)

            def attended_t(u, g):
                pe.wait_ge(s["on_ok"], g + 1)
                transposed(at[u][1], on[u], GROUPS * HALF, "oT_ps")

            def o_proj(u, g):
                pe.wait_ge(s["oT_ok"], g + 1)
                product(at[u][0][:, 0:D], list(zip(blocks_of(oT[u], KD), [wo[:, k, :] for k in range(KD)]))).then_inc(s["o_ps"], 1)

            def xn2_t(u, g):
                pe.wait_ge(s["xn2_ok"], g + 1)
                transposed(at[u][1], xn2[u], KD, "xn2T_ps")

            def gate(u, g):
                pe.wait_ge(s["xn2T_ok"], g + 1)
                product(at[u][0][:, 0:P], list(zip(blocks_of(gxT[u], KD), [wgs[:, k, 0:P] for k in range(KD)]))).then_inc(s["g_ps"], 1)

            def slot(i, c):
                now = stages(i, c)
                if "project" in now:
                    a, ua, na = now["project"]
                    embed(ua, a, na, c == -3)
                if "gate" in now:
                    p, up, _ = now["gate"]
                    gate(up, p)
                if c == TILES:
                    shared_up(2, 1)
                if "attend" in now:
                    q, uq, nq = now["attend"]
                    values(uq, q, nq, (0, ))
                if "spread" in now:
                    k, uk, _ = now["spread"]
                    latent_t(uk, k)
                if "attend" in now:
                    values(uq, q, nq, (1, 2))
                if "spread" in now:
                    values_t(uk, k)
                if "attend" in now:
                    scores(uq, q)
                    values(uq, q, nq, (3,))
                if "close" in now:
                    o, uo, _ = now["close"]
                    attended_t(uo, o)
                if "spread" in now:
                    keys(uk, k)
                if "project" in now:
                    xn_t(ua, a, na)
                if c == TILES - 2:
                    shared_t(0)
                if c == TILES - 1:
                    shared_t(1)
                if "close" in now:
                    o_proj(uo, o)
                if c in (TILES - 3, TILES - 2):
                    shared_up(c - (TILES - 3), 0)
                if c == TILES - 1:
                    shared_down(1)
                    shared_up(2, 0)
                if "project" in now:
                    q_latent(ua, a)
                if "attend" in now:
                    exps_t(uq, q)
                if "spread" in now:
                    k_t(uk, k)
                if c in (TILES - 3, TILES - 2):
                    shared_up(c - (TILES - 3), 1)
                if "spread" in now:
                    q_t(uk, k)
                if "attend" in now:
                    attend(uq, q)
                if "close" in now:
                    xn2_t(uo, o)
                if c == TILES - 2:
                    shared_down(0)
                if c == -1:
                    pe.wait_ge(s["ld_o"], 16)
                    pe.wait_ge(s["ld_s"], 32)

            def shared_up(g, n):
                u = g % 2
                if n == 0:
                    pe.wait_ge(s["xn2T_kept"], g + 1)
                    if g < 2:
                        pe.wait_ge(s["qT_ok"], TILES - 1 + g)
                        pe.wait_ge(s["kx_ok"], 2 * (TILES - 1 + g))
                    elif g < 4:
                        pe.wait_ge(s["acc_ok"], g - 1)
                    else:
                        pe.wait_ge(s["sh_ok"], g - 1)
                m = product(pj[u][n][:], [(xn2T[:, g, k * P:(k + 1) * P], wgs[:, k, E + n * SINTER:E + (n + 1) * SINTER])
                                          for k in range(KD)])
                if n == 1:
                    m.then_inc(s["sh_ps"], 1)

            def shared_t(g):
                pe.wait_ge(s["sh_ok"], g + 1)
                if 2 <= g < 4:
                    pe.wait_ge(s["lg_ok"], TILES - 3 + g)
                elif g >= 4:
                    pe.wait_ge(s["hsT_ok"], g - 1)
                transposed(shared_banks(g)[0], hs[g % 2], KS, "hsT_ps")

            def shared_down(g):
                pe.wait_ge(s["hsT_ok"], g + 1)
                if g > 2:
                    pe.wait_ge(s["acc_ok"], g)
                product(shared_banks(g)[1][:, 0:D], [(hsT[g % 2][:, k * P:(k + 1) * P], ws2[:, k, :]) for k in range(KS)])\
                    .then_inc(s["z_ps"], 1)

            pe.wait_ge(s["ld_emb0"], 16)
            slots(pe, slot)

            def shared_up2(g):
                shared_up(g, 0)
                shared_up(g, 1)

            shared_up2(3)
            pe.wait_ge(s["route"], 13)
            product(bank[7][:, 0:G], [(cst[:, C_TRI:C_TRI + P], rt[:, 5, :])])
            product(bank[7][:, G:2 * G], [(cst[:, C_ONE:C_ONE + P], rt[:, 5, :])]).then_inc(s["cnt_ps"], 1)
            shared_t(2)
            shared_up2(4)
            shared_down(2)
            shared_t(3)
            shared_up2(5)
            pe.wait_ge(s["lanes"], 3)
            for ch in range(NCH):
                if ch % 4 == 0:
                    pe.wait_ge(s["lanes"], 4 + ch // 4)
                m = nc.tensor.matmul(bank[7][:, 256:256 + 4 * SLOT_TILES], lane1[ch // 4][:, ch % 4, :],
                                     what[:, ch * 2 * SLOT_TILES:(ch + 2) * 2 * SLOT_TILES], start=ch == 0, stop=ch == NCH - 1)
            m.then_inc(s["tab_ps"], 1)
            shared_down(3)
            shared_t(4)
            for g in range(6, TILES):
                shared_up2(g)
                shared_down(g - 2)
                shared_t(g - 1)
            shared_down(TILES - 2)
            shared_t(TILES - 1)

            def gathered(t, u):
                pe.wait_ge(gat[u % RING], t * (16 // RING) + 16 * (1 + u // RING))
                transposed(bank[u % 2], xg[u % RING], KD, "xgT_ps")

            expert_reg = [pe.alloc_register(f"expert{n}") for n in range(RING + 2)]

            def experts_of(t, first, last):
                lo, hi = 0 if first else -1, RING if last else RING + 1
                regs = expert_reg[0:hi - lo]
                pe.load(regs, ti[0:1, t + lo:t + hi] if isinstance(t, int) else ti[0:1, bass.ds(t + lo, hi - lo)])
                return {u: pe.snap(r, min_val=0, max_val=E - 1) for u, r in zip(range(lo, hi), regs)}

            def of_expert(e, high, low, n):
                blocks = [[w[:, e, k * n:(k + 1) * n] for k in range(KD)] for w in (high, low)]
                return [(0, k, blocks[0][k]) for k in range(KD)] + [(0, k, blocks[1][k]) for k in range(KD)] \
                    + [(1, k, blocks[0][k]) for k in range(KD)]

            def split_product(dst, x, weights):
                return product(dst, [(x[:, part, k * P:(k + 1) * P], w) for part, k, w in weights])

            def up_weights(e):
                return of_expert(e, we13h, we13l, 2 * INTER)

            def down_weights(e):
                return of_expert(e, we2h, we2l, D)

            def up(t, u, weights):
                j, b = t + u, u % 2
                pe.wait_ge(s["xgT_ok"], j + 1)
                split_product(bank[2 + b][:], xgT[b], weights).then_inc(s["eh_ps"], 1)

            def hidden(t, u):
                pe.wait_ge(s["eh_ok"], t + u + 1)
                transposed(bank[4 + u % 2], eh[u % 2], KI, "ehT_ps")

            def down(t, u, weights):
                j, b = t + u, u % 2
                pe.wait_ge(s["ehT_ok"], j + 1)
                split_product(bank[6 + b][:, 0:D], ehT[b], weights).then_inc(s["y_ps"], 1)

            def experts(t, first=False, last=False):
                if first:
                    gathered(0, 0)
                    gathered(0, 1)
                    shared_down(TILES - 1)
                    pe.wait_ge(s["w_low"], E)
                    pe.wait_ge(s["w_low2"], len(weight_blocks()) - E)
                    pe.wait_ge(s["et_ok"], 1)
                of = experts_of(t, first, last)
                if first:
                    up(0, 0, up_weights(of[0]))
                    gathered(0, 2)
                for u in range(RING):
                    if u == 0:
                        w_up = up_weights(of[1])
                    if not (last and u == RING - 1):
                        up(t, u + 1, w_up)
                    if not (first and u == 0):
                        w_down = down_weights(of[u - 1])
                    if not (last and u >= RING - 3):
                        gathered(t, u + 3)
                    if u < RING - 2 or (u == RING - 2 and not last):
                        w_up = up_weights(of[u + 2])
                    hidden(t, u)
                    if not (first and u == 0):
                        down(t, u - 1, w_down)
                if last:
                    down(t, RING - 1, down_weights(of[RING - 1]))

            experts(0, first=True)
            with pe.Fori(RING, SLOT_TILES - RING, RING) as t:
                experts(t)
            experts(SLOT_TILES - RING, last=True)


def constants():
    c = np.zeros((P, C_END), np.float32)
    p = np.arange(P)
    c[:, C_ID:C_ID + P] = np.eye(P)
    c[:, C_TRI:C_TRI + P] = p[:, None] < p[None, :]
    c[:, C_ONE:C_ONE + P] = 1.0
    half = HD // 2
    inv = (1.0 / np.float32(10000.0) ** (np.arange(half, dtype=np.float32) / np.float32(half))).astype(np.float32)
    ang = (p % T).astype(np.float32)[:, None] * inv[None, :]
    cos, sin = np.cos(ang), np.sin(ang)
    both = np.concatenate([cos, cos], 1)
    cross = np.concatenate([sin, -sin], 1)
    scale = 1.0 / np.sqrt(HD)
    c[:, C_CQ:C_CQ + HD], c[:, C_SQ:C_SQ + HD] = both * scale, cross * scale
    c[:, C_CK:C_CK + HD], c[:, C_SK:C_SK + HD] = both, cross
    c[:, C_CAUSAL:C_CAUSAL + T] = np.where(np.arange(T)[None, :] <= (p % T)[:, None], 0.0, -3.0e38)
    e = np.arange(E)
    c[:, C_LT:C_LT + E * E] = (e[None, :] < e[:, None]).reshape(-1)
    c[:, C_THR:C_THR + E] = P * e
    c[:, C_TILE:C_TILE + SLOT_TILES] = np.arange(SLOT_TILES)
    c[:, C_MHALF] = -0.5
    c[:, C_HEAD:C_HEAD + HPH] = p[:, None] // HD == np.arange(HPH)[None, :]
    c[:, C_IOTA:C_IOTA + P] = p
    token = np.arange(TILES)[None, :] * P + p[:, None]
    for k in range(TOPK):
        c[:, C_ROW + k * TILES:C_ROW + (k + 1) * TILES] = token * TOPK + k + 1
    c[:, C_PAD:C_PAD + SLOT_TILES] = TOKENS * TOPK + p[:, None] + P * np.arange(SLOT_TILES)[None, :] + 1
    return c


def kernel(x, L0_tok_W, L0_tok_b, L0_tok_pos_emb, L0_attn_W_q, L0_attn_W_dkv, L0_attn_W_uk, L0_attn_W_uv, L0_attn_W_o,
           L0_attn_ln_gamma, L0_attn_ln_beta, L0_ffn_gate_w, L0_ffn_gate_bias, L0_ffn_w1, L0_ffn_w3, L0_ffn_w2,
           L0_ffn_sw1, L0_ffn_sw3, L0_ffn_sw2):
    import concourse.bacc as bacc
    from concourse.bass_utils import run_bass_kernel_spmd

    a = np.asarray

    def blocks(w, k):
        w = a(w)
        return np.ascontiguousarray(w.reshape(k, P, -1).transpose(1, 0, 2).reshape(P, -1))

    def spread(v):
        return np.broadcast_to(a(v)[None, :], (P, a(v).shape[0]))

    xs = a(x).reshape(TILES, IPT, CH, NP, PS, NP, PS).transpose(0, 2, 4, 6, 1, 3, 5).reshape(TILES, KF, P, P)
    ins = {
        "xp": np.ascontiguousarray(xs.transpose(0, 2, 1, 3).reshape(TILES, P, KF * P)),
        "w_emb": blocks(a(L0_tok_W).T, KF),
        "w_qd": blocks(np.concatenate([a(L0_attn_W_q), a(L0_attn_W_dkv)], 1), KD),
        "w_kv": np.ascontiguousarray(np.concatenate([a(L0_attn_W_uk), a(L0_attn_W_uv)], 1)),
        "w_o": blocks(L0_attn_W_o, KD),
        "w_gs": blocks(np.concatenate([a(L0_ffn_gate_w).T, a(L0_ffn_sw1).T, a(L0_ffn_sw3).T], 1), KD),
        "w_s2": blocks(a(L0_ffn_sw2).T, KS),
        "w_e13": np.stack([blocks(np.concatenate([a(L0_ffn_w1)[e].T, a(L0_ffn_w3)[e].T], 1), KD) for e in range(E)]),
        "w_e2": np.stack([blocks(a(L0_ffn_w2)[e].T, KI) for e in range(E)]),
        "rows": np.ascontiguousarray(np.concatenate(
            [np.tile(a(L0_tok_pos_emb), (IPT, 1)), spread(L0_tok_b), spread(L0_attn_ln_gamma), spread(L0_attn_ln_beta),
             spread(L0_ffn_gate_bias)], 1)),
        "consts": constants(),
    }
    nc = bacc.Bacc("TRN2", target_bir_lowering=False, num_devices=1)
    args = [nc.dram_tensor(n, v.shape, mybir.dt.from_np(v.dtype), kind="ExternalInput").ap() for n, v in ins.items()]
    args.append(nc.dram_tensor("out", (TOKENS, D), F32, kind="ExternalOutput").ap())
    build(nc, *args)
    r = run_bass_kernel_spmd(nc, [ins], core_ids=[0])
    return r.results[0]["out"].reshape(IMAGES, T, D)
```
